# Optimizing a Trainium2 kernel written in Bass

```python
import numpy as np
import jax
import jax.numpy as jnp

def _softmax(x, axis=-1):
    return jax.nn.softmax(x, axis=axis)

def _gelu(x):
    return jax.nn.gelu(x, approximate=True)

def _silu(x):
    return jax.nn.silu(x)

def _sigmoid(x):
    return jax.nn.sigmoid(x)

def _layernorm(x, axis=-1, eps=1e-05):
    m = jnp.mean(x, axis=axis, keepdims=True)
    v = jnp.var(x, axis=axis, keepdims=True)
    return (x - m) / jnp.sqrt(v + eps)

def _scatter_add(tgt, idx, src, axis=0):
    return tgt.at[idx].add(src)

def _segment_sum(src, seg, n):
    return jax.ops.segment_sum(src, seg, n)
kernel_name = 'mk_gnn_resnorm_d2_gnn_r32_cb7a3f'

def setup_inputs(seed: int=0):
    np.random.seed(seed)
    _w = jnp.asarray

    def _rec_inputs():
        import jax
        import jax.numpy as jnp
        _gk = jax.random.key(seed)
        x = -0.0005121 + 1.001 * jax.random.normal(jax.random.fold_in(_gk, 1), (3125, 64), jnp.float32)
        _s = jax.random.randint(jax.random.fold_in(_gk, 2), (50000,), 0, 3125, jnp.int32)
        _d = jax.random.randint(jax.random.fold_in(_gk, 3), (50000,), 0, 3125, jnp.int32)
        _loop = jnp.arange(3125, dtype=jnp.int32)
        src = jnp.concatenate([_s, _d, _loop])
        dst = jnp.concatenate([_d, _s, _loop])
        _o = jnp.argsort(dst, stable=True)
        src = src[_o]
        dst = dst[_o]
        edge_attr_32 = 0.000283511 + 1.00007 * jax.random.normal(jax.random.fold_in(_gk, 12), (103125, 32), jnp.float32)
        return (x, src, dst, edge_attr_32)
    x, src, dst, edge_attr_32 = _rec_inputs()

    def _L0_gnn_setup():
        import math
        import jax, jax.numpy as jnp
        import numpy as np
        N_NODES = 50000
        N_EDGES = 18750
        IN_CH = 64
        HEADS = 2
        C = 64
        HC = HEADS * C
        EDGE_DIM = 32

        def _layernorm(x, g, b, eps=1e-05):
            m = jnp.mean(x, axis=-1, keepdims=True)
            v = jnp.mean(jnp.square(x - m), axis=-1, keepdims=True)
            return (x - m) / jnp.sqrt(v + eps) * g + b
        key = jax.random.key(seed)
        ks = jax.random.split(key, 12)
        s = 0.05
        return {'x': jax.random.normal(ks[0], (N_NODES, IN_CH), jnp.float32), 'edge_index': jax.random.randint(ks[1], (2, N_EDGES), 0, N_NODES, dtype=jnp.int64), 'edge_attr': jax.random.normal(ks[2], (N_EDGES, EDGE_DIM), jnp.float32), 'Wq': s * jax.random.normal(ks[3], (IN_CH, HC), jnp.float32), 'bq': jnp.zeros((HC,), jnp.float32), 'Wk': s * jax.random.normal(ks[4], (IN_CH, HC), jnp.float32), 'bk': jnp.zeros((HC,), jnp.float32), 'Wv': s * jax.random.normal(ks[5], (IN_CH, HC), jnp.float32), 'bv': jnp.zeros((HC,), jnp.float32), 'We': s * jax.random.normal(ks[6], (EDGE_DIM, HC), jnp.float32), 'Wp': s * jax.random.normal(ks[7], (HC, IN_CH), jnp.float32), 'bp': jnp.zeros((IN_CH,), jnp.float32), 'ln1_g': jnp.ones((IN_CH,), jnp.float32), 'ln1_b': jnp.zeros((IN_CH,), jnp.float32), 'ln2_g': jnp.ones((IN_CH,), jnp.float32), 'ln2_b': jnp.zeros((IN_CH,), jnp.float32), 'W1': s * jax.random.normal(ks[8], (IN_CH, IN_CH), jnp.float32), 'b1': jnp.zeros((IN_CH,), jnp.float32), 'W2': s * jax.random.normal(ks[9], (IN_CH, IN_CH), jnp.float32), 'b2': jnp.zeros((IN_CH,), jnp.float32)}
    _L0_gnn_all = _L0_gnn_setup()
    _L0_gnn_in = {k: v for k, v in _L0_gnn_all.items() if k in ('Wq', 'bq', 'Wk', 'bk', 'Wv', 'bv', 'We', 'Wp', 'bp', 'ln1_g', 'ln1_b', 'ln2_g', 'ln2_b', 'W1', 'b1', 'W2', 'b2')}
    del _L0_gnn_all

    def _L1_gnn_setup():
        import jax, jax.numpy as jnp
        import numpy as np
        N_NODES = 50000
        N_EDGES = 25000
        D_NODE = 64
        D_EDGE = 32
        D_HID = 128

        def _mlp(x, W1, b1, W2, b2):
            return jax.nn.relu(x @ W1 + b1) @ W2 + b2
        key = jax.random.key(seed)
        ks = jax.random.split(key, 12)
        inp = {'nodes': jax.random.normal(ks[0], (N_NODES, D_NODE), dtype=jnp.float32), 'row': jax.random.randint(ks[1], (N_EDGES,), 0, N_NODES, dtype=jnp.int32), 'col': jax.random.randint(ks[2], (N_EDGES,), 0, N_NODES, dtype=jnp.int32), 'edge_features': jax.random.normal(ks[3], (N_EDGES, D_EDGE), dtype=jnp.float32)}
        d_in_msg = 2 * D_NODE + D_EDGE
        inp['mW1'] = jax.random.normal(ks[4], (d_in_msg, D_HID), dtype=jnp.float32) / np.sqrt(d_in_msg)
        inp['mb1'] = jnp.zeros((D_HID,), dtype=jnp.float32)
        inp['mW2'] = jax.random.normal(ks[5], (D_HID, D_NODE), dtype=jnp.float32) / np.sqrt(D_HID)
        inp['mb2'] = jnp.zeros((D_NODE,), dtype=jnp.float32)
        d_in_upd = 2 * D_NODE
        inp['uW1'] = jax.random.normal(ks[6], (d_in_upd, D_HID), dtype=jnp.float32) / np.sqrt(d_in_upd)
        inp['ub1'] = jnp.zeros((D_HID,), dtype=jnp.float32)
        inp['uW2'] = jax.random.normal(ks[7], (D_HID, D_NODE), dtype=jnp.float32) / np.sqrt(D_HID)
        inp['ub2'] = jnp.zeros((D_NODE,), dtype=jnp.float32)
        return inp
    _L1_gnn_all = _L1_gnn_setup()
    _L1_gnn_in = {k: v for k, v in _L1_gnn_all.items() if k in ('mW1', 'mb1', 'mW2', 'mb2', 'uW1', 'ub1', 'uW2', 'ub2')}
    del _L1_gnn_all
    return {'x': x, 'src': src, 'dst': dst, 'edge_attr_32': edge_attr_32, 'L0_gnn_Wq': _L0_gnn_in['Wq'], 'L0_gnn_bq': _L0_gnn_in['bq'], 'L0_gnn_Wk': _L0_gnn_in['Wk'], 'L0_gnn_bk': _L0_gnn_in['bk'], 'L0_gnn_Wv': _L0_gnn_in['Wv'], 'L0_gnn_bv': _L0_gnn_in['bv'], 'L0_gnn_We': _L0_gnn_in['We'], 'L0_gnn_Wp': _L0_gnn_in['Wp'], 'L0_gnn_bp': _L0_gnn_in['bp'], 'L0_gnn_ln1_g': _L0_gnn_in['ln1_g'], 'L0_gnn_ln1_b': _L0_gnn_in['ln1_b'], 'L0_gnn_ln2_g': _L0_gnn_in['ln2_g'], 'L0_gnn_ln2_b': _L0_gnn_in['ln2_b'], 'L0_gnn_W1': _L0_gnn_in['W1'], 'L0_gnn_b1': _L0_gnn_in['b1'], 'L0_gnn_W2': _L0_gnn_in['W2'], 'L0_gnn_b2': _L0_gnn_in['b2'], 'L1_gnn_mW1': _L1_gnn_in['mW1'], 'L1_gnn_mb1': _L1_gnn_in['mb1'], 'L1_gnn_mW2': _L1_gnn_in['mW2'], 'L1_gnn_mb2': _L1_gnn_in['mb2'], 'L1_gnn_uW1': _L1_gnn_in['uW1'], 'L1_gnn_ub1': _L1_gnn_in['ub1'], 'L1_gnn_uW2': _L1_gnn_in['uW2'], 'L1_gnn_ub2': _L1_gnn_in['ub2']}

def reference(x, src, dst, edge_attr_32, L0_gnn_Wq, L0_gnn_bq, L0_gnn_Wk, L0_gnn_bk, L0_gnn_Wv, L0_gnn_bv, L0_gnn_We, L0_gnn_Wp, L0_gnn_bp, L0_gnn_ln1_g, L0_gnn_ln1_b, L0_gnn_ln2_g, L0_gnn_ln2_b, L0_gnn_W1, L0_gnn_b1, L0_gnn_W2, L0_gnn_b2, L1_gnn_mW1, L1_gnn_mb1, L1_gnn_mW2, L1_gnn_mb2, L1_gnn_uW1, L1_gnn_ub1, L1_gnn_uW2, L1_gnn_ub2):
    import jax
    import jax.numpy as jnp

    def _L0_gnn_ref(x, edge_index, edge_attr, Wq, bq, Wk, bk, Wv, bv, We, Wp, bp, ln1_g, ln1_b, ln2_g, ln2_b, W1, b1, W2, b2):
        import math
        import jax, jax.numpy as jnp
        import numpy as np
        N_NODES = 50000
        N_EDGES = 18750
        IN_CH = 64
        HEADS = 2
        C = 64
        HC = HEADS * C
        EDGE_DIM = 32

        def _layernorm(x, g, b, eps=1e-05):
            m = jnp.mean(x, axis=-1, keepdims=True)
            v = jnp.mean(jnp.square(x - m), axis=-1, keepdims=True)
            return (x - m) / jnp.sqrt(v + eps) * g + b
        n = x.shape[0]
        residual = x
        h = _layernorm(x, ln1_g, ln1_b)
        q = (h @ Wq + bq).reshape(n, HEADS, C)
        k = (h @ Wk + bk).reshape(n, HEADS, C)
        v = (h @ Wv + bv).reshape(n, HEADS, C)
        src, tgt = (edge_index[0], edge_index[1])
        e = (edge_attr @ We).reshape(-1, HEADS, C)
        qi = q[tgt]
        kj = k[src] + e
        vj = v[src] + e
        alpha = jnp.sum(qi * kj, axis=-1) / math.sqrt(C)
        amax = jax.ops.segment_max(alpha, tgt, num_segments=n)
        ex = jnp.exp(alpha - amax[tgt])
        den = jax.ops.segment_sum(ex, tgt, num_segments=n)
        a = ex / (den[tgt] + 1e-08)
        agg = jax.ops.segment_sum(a[:, :, None] * vj, tgt, num_segments=n)
        out = agg.reshape(n, HC) @ Wp + bp
        out = out + residual
        res2 = out
        o = _layernorm(out, ln2_g, ln2_b)
        o = jax.nn.gelu(o @ W1 + b1, approximate=False) @ W2 + b2
        return o + res2

    def _L1_gnn_ref(nodes, row, col, edge_features, mW1, mb1, mW2, mb2, uW1, ub1, uW2, ub2):
        import jax, jax.numpy as jnp
        import numpy as np
        N_NODES = 50000
        N_EDGES = 25000
        D_NODE = 64
        D_EDGE = 32
        D_HID = 128

        def _mlp(x, W1, b1, W2, b2):
            return jax.nn.relu(x @ W1 + b1) @ W2 + b2
        msg_in = jnp.concatenate([nodes[row], nodes[col], edge_features], axis=-1)
        messages = _mlp(msg_in, mW1, mb1, mW2, mb2)
        aggregated = jax.ops.segment_sum(messages, col, num_segments=nodes.shape[0])
        upd_in = jnp.concatenate([nodes, aggregated], axis=-1)
        return _mlp(upd_in, uW1, ub1, uW2, ub2)
    edge_index = jnp.stack([src, dst])
    x = _layernorm(x + _L0_gnn_ref(x, edge_index, edge_attr_32, L0_gnn_Wq, L0_gnn_bq, L0_gnn_Wk, L0_gnn_bk, L0_gnn_Wv, L0_gnn_bv, L0_gnn_We, L0_gnn_Wp, L0_gnn_bp, L0_gnn_ln1_g, L0_gnn_ln1_b, L0_gnn_ln2_g, L0_gnn_ln2_b, L0_gnn_W1, L0_gnn_b1, L0_gnn_W2, L0_gnn_b2), axis=-1)
    x = _layernorm(x + _L1_gnn_ref(x, src, dst, edge_attr_32, L1_gnn_mW1, L1_gnn_mb1, L1_gnn_mW2, L1_gnn_mb2, L1_gnn_uW1, L1_gnn_ub1, L1_gnn_uW2, L1_gnn_ub2), axis=-1)
    return x

_drawn_inputs = setup_inputs


def setup_inputs(seed=0):
    import zlib

    import numpy as np

    out = dict(_drawn_inputs(seed))
    spreads = {'L0_gnn_bq': (0.0, 0.8),
     'L0_gnn_bk': (0.0, 2.0),
     'L0_gnn_bv': (0.0, 0.289),
     'L0_gnn_bp': (0.0, 0.314),
     'L0_gnn_ln1_g': (1.0, 0.6),
     'L0_gnn_ln1_b': (0.0, 0.686),
     'L0_gnn_ln2_g': (1.0, 0.6),
     'L0_gnn_ln2_b': (0.0, 2.0),
     'L0_gnn_b1': (0.0, 0.628),
     'L0_gnn_b2': (0.0, 0.1),
     'L1_gnn_mb1': (0.0, 0.1),
     'L1_gnn_mb2': (0.0, 0.1),
     'L1_gnn_ub1': (0.0, 0.8),
     'L1_gnn_ub2': (0.0, 0.611)}
    factors = {'L0_gnn_Wq': 8.0, 'L0_gnn_Wk': 8.0, 'L0_gnn_Wv': 3.227, 'L0_gnn_We': 5.675}
    for name, (base, spread) in spreads.items():
        noise = np.random.default_rng([zlib.crc32(name.encode()), seed]).standard_normal(out[name].shape)
        drawn = base * np.exp(spread * noise) if base else spread * noise
        out[name] = jnp.asarray(drawn.astype(out[name].dtype))
    for name, factor in factors.items():
        out[name] = (out[name] * factor).astype(out[name].dtype)
    return out
```

```python
from contextlib import ExitStack

import concourse.bass as bass
from concourse import mybir

F32 = mybir.dt.float32
I32 = mybir.dt.int32
U32 = mybir.dt.uint32
ALU = mybir.AluOpType
ACT = mybir.ActivationFunctionType
AX = mybir.AxisListType

P = 128
NODES = 3125
EDGES = 103125
D = 64
ED = 32
HEADS = 2
HC = HEADS * D
HID = 128
EPS = 1e-5

NT = -(-NODES // P)
FULL_T = NODES // P
LAST_N = NODES - FULL_T * P
NP = NT * P
CHUNK = 512
CHUNKS = [(c, min(c + CHUNK, NP)) for c in range(0, NP, CHUNK)]

J = 4
GE = P * J
G = -(-EDGES // GE)
EP = G * GE
W = 32
NO_NODE = 1 << 20
LAST_BASE = NP - W
assert LAST_BASE >= NODES
HW = HEADS * W

RING = 8
STEPS = (G - 2) // RING
assert G == STEPS * RING + 2 and RING % 2 == 0

ZF = D + ED + 1
FAR = 1e30
NO_MAX = -1e20


def slot(off):
    return off % RING


def uses(it, off):
    return it + off // RING


def at(it, off):
    return it * RING + off


def past(it, off, n):
    return not isinstance(it, int) or at(it, off) >= n


def build(nc, x, src, dst, ea, Wq, bq, Wk, bk, Wv, bv, We, Wp, bp, ln1_g, ln1_b, ln2_g, ln2_b, W1, b1, W2, b2,
          mW1, mb1, mW2, mb2, uW1, ub1, uW2, ub2, out):
    with ExitStack() as ctx:
        def sb(name, shape, dt=F32):
            return ctx.enter_context(nc.sbuf_tensor(name, shape, dt))

        def sem(name):
            return ctx.enter_context(nc.semaphore(name))

        source_rows = nc.dram_tensor("source_rows", (NP, D), F32).ap()
        query_cols = nc.dram_tensor("query_cols", (ZF, NP, HEADS), F32).ap()
        target_rows = nc.dram_tensor("target_rows", (NP, HID), F32).ap()
        lohi_dram = nc.dram_tensor("lohi_dram", (2, G), F32).ap()

        ident = sb("ident", [P, P])
        ones = sb("ones", [P, 1])
        node_id = sb("node_id", [P, NP])
        X = sb("X", [P, NT, D])
        H = sb("H", [P, NT, D])
        T = sb("T", [P, NT, D])
        RES = sb("RES", [P, NT, D])
        stat = sb("stat", [P, 4, NT])
        rows = sb("rows", [P, 6, D])
        nodesT = sb("nodesT", [D + 1, NP])
        nodesT2 = sb("nodesT2", [D + 1, NP])
        queryT = sb("queryT", [P, NP, HEADS])
        best = sb("best", [P, HEADS, NP])
        acc = sb("acc", [P, HEADS, NP])
        base0 = sb("base0", [1, 2, G])
        base_f = sb("base_f", [1, G])
        base_i = sb("base_i", [1, G], I32)
        span = sb("span", [1, 2])
        rounds_i = sb("rounds_i", [1, 2], I32)
        WqB = sb("WqB", [D + 1, HC])
        Wkc = sb("Wkc", [ZF, HC])
        Wvc = sb("Wvc", [ZF, HC])
        WkcT = sb("WkcT", [P, ZF])
        WvcT = sb("WvcT", [P, ZF])
        WpS = sb("WpS", [P, D])
        U = sb("U", [ZF, HEADS, D + 1])
        W1B = sb("W1B", [D + 1, D])
        W2B = sb("W2B", [D + 1, D])
        mWB = sb("mWB", [D + 1, HID])
        mW2S = sb("mW2S", [P, D])
        mb2S = sb("mb2S", [1, D])
        uWA = sb("uWA", [D + 1, HID])
        uWB = sb("uWB", [D, HID])
        uW2S = sb("uW2S", [P, D])
        idx = sb("idx", [P, RING, J], I32)
        tgt = sb("tgt", [P, RING, J], I32)
        z = sb("z", [P, RING, J, P])
        zT = sb("zT", [P, 2, GE])
        other = sb("other", [P, 2, J, W])
        SM = sb("SM", [P, 2, HEADS, J, W])
        folded = sb("folded", [P, 2, P])
        Qw = sb("Qw", [ZF, RING, W, HEADS])
        colmax = sb("colmax", [HW, 2])
        mnew = sb("mnew", [P, HEADS, W])
        XE = sb("XE", [P, 2, HEADS * J * W + HW])
        E = sb("E", [P, 2, HEADS * J * W + HW])
        kept = sb("kept", [P, HEADS, W])
        Wg = sb("Wg", [P, RING, HID])
        hid = sb("hid", [P, 2, J, HID])
        cnt = sb("cnt", [1, NP])

        qT = best[:, 0, 0:2 * CHUNK].rearrange("p (a n) -> p a n", a=2)
        ids = best[:, 1, :].bitcast(I32)
        heads_out = best[:, :, :].rearrange("p h n -> p (h n)")[:, 0:NT * HEADS * (D + 1)].rearrange(
            "p (t h d) -> p t h d", t=NT, h=HEADS)
        dst_rows = acc[:, :, :].rearrange("p h n -> p (h n)")[0:G // 2, 0:2 * GE].bitcast(I32).rearrange(
            "p (a e) -> p a e", a=2)
        dst_real = acc[:, :, :].rearrange("p h n -> p (h n)")[0:G // 2, 2 * GE:4 * GE].rearrange(
            "p (a e) -> p a e", a=2)
        lohi = stat[0:G // 2, 0:1, 0:4].rearrange("p a (k b) -> p (a k) b", k=2)
        R_out = acc[:, 0, :].rearrange("p (t n) -> p t n", t=NT)
        queryT_flat = queryT[:, :, :].rearrange("p n h -> p (n h)")
        msgT = queryT_flat[:, 0:NP]
        hidT = queryT_flat[:, NP:]

        def psum(name, shape):
            return nc.psum_tensor(name, shape, F32)

        def wide(row, shape):
            return row.broadcast_to(shape)

        s_w = sem("weights_in")
        s_x = sem("x_in")
        s_xpad = sem("x_padding_zeroed")
        s_onerow = sem("ones_rows_set")
        s_wrows = sem("weight_rows_in")
        s_ident0 = sem("ident_cleared")
        s_ident = sem("ident_ready")
        s_ids = sem("ids_ready")
        s_dve = sem("vector_step")
        s_var = sem("variance_ready")
        s_std = sem("deviation_ready")
        s_h = sem("normalized_ready")
        s_tp = sem("transposed")
        s_tc = sem("transpose_copied")
        s_q = sem("query_product")
        s_qc = sem("query_copied")
        s_qq = sem("score_product")
        s_qqc = sem("score_copied")
        s_wt = sem("weights_transposed")
        s_wtc = sem("weights_transpose_copied")
        s_dst = sem("dst_rows_in")
        s_lohi = sem("lohi_ready")
        s_lod = sem("lohi_out")
        s_lor = sem("lohi_row_in")
        s_tab = sem("source_rows_out")

        steps = [0]

        def link(eng, ins):
            steps[0] += 1
            ins.then_inc(s_dve, 1)
            eng.wait_ge(s_dve, steps[0])

        def normalize(dve, a, b, scratch, turn):
            mean, rstd = stat[:, 0, :], stat[:, 1, :]
            link(dve, nc.vector.tensor_reduce(mean, a, AX.X, ALU.add))
            link(dve, nc.vector.tensor_scalar(mean, mean, 1.0 / D, None, ALU.mult))
            link(dve, nc.vector.tensor_tensor(b, a, wide(mean.unsqueeze(2), [P, NT, D]), ALU.subtract))
            link(dve, nc.vector.tensor_tensor(scratch, b, b, ALU.mult))
            link(dve, nc.vector.tensor_reduce(rstd, scratch, AX.X, ALU.add))
            nc.vector.tensor_scalar(stat[:, 2, :], rstd, 1.0 / D, EPS, ALU.mult, ALU.add).then_inc(s_var, 1)
            dve.wait_ge(s_std, turn)
            link(dve, nc.vector.reciprocal(rstd, stat[:, 3, :]))
            return nc.vector.tensor_tensor(b, b, wide(rstd.unsqueeze(2), [P, NT, D]), ALU.mult)

        def deviation(act, turn):
            act.wait_ge(s_var, turn)
            nc.scalar.activation(stat[:, 3, :], stat[:, 2, :], ACT.Sqrt).then_inc(s_std, 1)

        def scale_shift(dve, a, k):
            link(dve, nc.vector.tensor_tensor(a, a, wide(rows[:, k:k + 1, :], [P, NT, D]), ALU.mult))
            return nc.vector.tensor_tensor(a, a, wide(rows[:, k + 1:k + 2, :], [P, NT, D]), ALU.add)

        def spread(row):
            return row.rearrange("(a d) -> a d", a=1).partition_broadcast(P)

        n_w = 22
        with psum("pT", [D, 2, CHUNK]) as pT, psum("pW", [P, 2, CHUNK]) as pW, psum("pQ", [P, CHUNK]) as pQ, \
                psum("pS", [P, 2, CHUNK]) as pS, nc.Block() as block:

            @block.sync
            def _(sp):
                sp.wait_ge(s_xpad, 1)
                sp.dma_start(X[:, 0:FULL_T, :], x[0:FULL_T * P, :].rearrange("(t p) d -> p t d", p=P)).then_inc(s_x, 16)
                sp.dma_start(X[0:LAST_N, FULL_T, :], x[FULL_T * P:NODES, :]).then_inc(s_x, 16)
                sp.dma_start(dst_rows, dst.rearrange("(p a e) -> p a e", a=2, e=GE)).then_inc(s_dst, 16)
                sp.wait_ge(s_lohi, 1)
                for k in range(2):
                    sp.dma_start(lohi_dram[k, :].rearrange("(p a) -> p a", a=2), lohi[:, k, :]).then_inc(s_lod, 16)
                sp.wait_ge(s_lod, 32)
                sp.dma_start(base0[:, :, :], lohi_dram.rearrange("(o k) g -> o k g", o=1)).then_inc(s_lor, 16)
                sp.wait_ge(s_h, 1)
                sp.dma_start(source_rows.rearrange("(t p) d -> p t d", p=P), H[:, :, :]).then_inc(s_tab, 16)
                for n, (a, b) in enumerate(CHUNKS):
                    sp.wait_ge(s_qqc, n + 1)
                    sp.dma_start(query_cols[:, a:b, :], queryT[0:ZF, a:b, :]).then_inc(s_tab, 16)
                sp.wait_ge(s_tab, 16 * (1 + len(CHUNKS)))

            @block.gpsimd
            def _(pool):
                nc.gpsimd.memset(ident[:, :], 0.0).then_inc(s_ident0, 1)
                pool.wait_ge(s_ident0, 1)
                nc.gpsimd.affine_select(out=ident[:, :], in_=ident[:, :], compare_op=ALU.not_equal, fill=1.0, base=0,
                                        pattern=[[-1, P]], channel_multiplier=1).then_inc(s_ident, 1)
                nc.gpsimd.iota(ids, [[1, NP]], base=0, channel_multiplier=0).then_inc(s_ids, 1)

            @block.scalar
            def _(act):
                loads = [(WqB[0:D, :], Wq), (WqB[D:D + 1, :], bq.rearrange("(a n) -> a n", a=1))]
                for tile, w, b in ((Wkc, Wk, bk), (Wvc, Wv, bv)):
                    loads += [(tile[0:D, :], w), (tile[D:D + ED, :], We),
                              (tile[D + ED:ZF, :], b.rearrange("(a n) -> a n", a=1))]
                loads += [(WpS[:, :], Wp)]
                for tile, w, b in ((W1B, W1, b1), (W2B, W2, b2), (mWB, mW1[D:2 * D, :], mb1), (uWA, uW1[0:D, :], ub1)):
                    loads += [(tile[0:D, :], w), (tile[D:D + 1, :], b.rearrange("(a n) -> a n", a=1))]
                loads += [(mW2S[:, :], mW2), (mb2S[:, :], mb2.rearrange("(a n) -> a n", a=1)),
                          (uWB[:, :], uW1[D:2 * D, :]), (uW2S[:, :], uW2)]
                loads += [(rows[:, k, :], spread(r)) for k, r in enumerate((ln1_g, ln1_b, ln2_g, ln2_b, bp, ub2))]
                for to, of in loads:
                    act.dma_start(to, of).then_inc(s_w, 16)
                assert len(loads) == WEIGHT_LOADS
                deviation(act, 1)
                for n, (a, b) in enumerate(CHUNKS):
                    act.wait_ge(s_tp, n + 1)
                    nc.scalar.copy(nodesT[0:D, a:b], pT[:, n % 2, 0:b - a]).then_inc(s_tc, 1)
                    act.wait_ge(s_q, n + 1)
                    if n >= 2:
                        act.wait_ge(s_qq, n - 1)
                    nc.scalar.mul(qT[:, n % 2, 0:b - a], pQ[:, 0:b - a], float(D) ** -0.5).then_inc(s_qc, 1)

            @block.vector
            def _(dve):
                nc.vector.memset(X[:, FULL_T, :], 0.0).then_inc(s_xpad, 1)
                nc.vector.memset(ones[:, :], 1.0)
                nc.vector.memset(folded[:, :, :], 0.0)
                nc.vector.memset(nodesT2[D:D + 1, :], 1.0)
                nc.vector.memset(z[:, :, :, :], 1.0)
                nc.vector.memset(nodesT[D:D + 1, :], 1.0).then_inc(s_onerow, 1)
                dve.wait_ge(s_x, 32)
                link(dve, normalize(dve, X[:, :, :], H[:, :, :], T[:, :, :], 1))
                dve.wait_ge(s_w, 16 * WEIGHT_LOADS)
                scale_shift(dve, H[:, :, :], 0).then_inc(s_h, 1)
                dve.wait_ge(s_ids, 1)
                link(dve, nc.vector.tensor_copy(node_id[:, :], ids))
                dve.wait_ge(s_dst, 16)
                link(dve, nc.vector.scalar_tensor_tensor(out=dst_real, in0=dst_rows, scalar=float(NO_NODE),
                                                         in1=dst_rows, op0=ALU.is_lt, op1=ALU.mult))
                nc.vector.tensor_reduce(lohi[:, 0, :], dst_rows, AX.X, ALU.min)
                link(dve, nc.vector.tensor_reduce(lohi[:, 1, :], dst_real, AX.X, ALU.max))
                dve.sem_inc(s_lohi, 1)
                dve.wait_ge(s_wt, 1)
                nc.vector.tensor_copy(WkcT[:, :], pW[:, 0, 0:ZF])
                nc.vector.tensor_copy(WvcT[:, :], pW[:, 1, 0:ZF]).then_inc(s_wtc, 1)
                for n, (a, b) in enumerate(CHUNKS):
                    dve.wait_ge(s_qq, n + 1)
                    nc.vector.tensor_copy(queryT[0:ZF, a:b, :].rearrange("p n h -> p h n"),
                                          pS[0:ZF, :, 0:b - a]).then_inc(s_qqc, 1)
                dve.wait_ge(s_wt, 2)
                link(dve, nc.vector.memset(U[:, :, :], 0.0))
                nc.vector.memset(U[ZF - 1:ZF, :, D:D + 1], 1.0)
                for h in range(HEADS):
                    nc.vector.tensor_copy(U[:, h, 0:D], pW[0:ZF, h, 0:D])
                dve.wait_ge(s_lor, 16)
                link(dve, nc.vector.tensor_tensor(base_f[:, :], base0[:, 1, :], base0[:, 0, :], ALU.subtract))
                link(dve, nc.vector.tensor_reduce(span[:, 0:1], base_f[:, :], AX.X, ALU.max))
                link(dve, nc.vector.tensor_copy(rounds_i[:, 0:1], span[:, 0:1]))
                link(dve, nc.vector.tensor_scalar(rounds_i[:, 0:1], rounds_i[:, 0:1], W.bit_length() - 1, None,
                                                  ALU.arith_shift_right))
                link(dve, nc.vector.tensor_scalar(rounds_i[:, 1:2], rounds_i[:, 0:1], 1.0, None, ALU.add))
                nc.vector.tensor_scalar(base_f[:, :], base0[:, 0, :], float(-W), None, ALU.add)
                nc.vector.memset(best[:, :, :], NO_MAX)
                nc.vector.memset(acc[:, :, :], 0.0)

            @block.tensor
            def _(pe):
                pe.wait_ge(s_w, 16 * WEIGHT_LOADS)
                pe.wait_ge(s_ident, 1)
                nc.tensor.transpose(pW[:, 0, 0:ZF], Wkc[:, :], ident[0:ZF, 0:ZF])
                nc.tensor.transpose(pW[:, 1, 0:ZF], Wvc[:, :], ident[0:ZF, 0:ZF]).then_inc(s_wt, 1)
                pe.wait_ge(s_h, 1)
                pe.wait_ge(s_onerow, 1)
                pe.wait_ge(s_wtc, 1)
                for n, (a, b) in enumerate(CHUNKS):
                    for t in range(a // P, b // P):
                        last = nc.tensor.transpose(pT[:, n % 2, t * P - a:t * P - a + P], H[:, t, :], ident[:, :])
                    last.then_inc(s_tp, 1)
                    pe.wait_ge(s_tc, n + 1)
                    nc.tensor.matmul(pQ[:, 0:b - a], WqB[:, :], nodesT[:, a:b], start=True, stop=True).then_inc(s_q, 1)
                    pe.wait_ge(s_qc, n + 1)
                    if n >= 1:
                        pe.wait_ge(s_qqc, n)
                    for h in range(HEADS):
                        last = nc.tensor.matmul(pS[0:ZF, h, 0:b - a], WkcT[h * D:(h + 1) * D, :],
                                                qT[h * D:(h + 1) * D, n % 2, 0:b - a], start=True, stop=True)
                    last.then_inc(s_qq, 1)
                for h in range(HEADS):
                    last = nc.tensor.matmul(pW[0:ZF, h, 0:D], WvcT[h * D:(h + 1) * D, :], WpS[h * D:(h + 1) * D, :],
                                            start=True, stop=True)
                last.then_inc(s_wt, 1)

        s_gath1 = [sem(f"gathered_{i}") for i in range(RING)]
        s_gath2 = [sem(f"gathered_again_{i}") for i in range(RING)]
        s_base = sem("bases_ready")
        s_idx = [sem(f"sources_in_{i}") for i in range(RING)]
        s_tgt = [sem(f"targets_in_{i}") for i in range(RING)]
        s_ea = [sem(f"edge_features_in_{i}") for i in range(RING)]
        s_win = [sem(f"target_window_in_{i}") for i in range(RING)]
        s_turn = sem("gather_turn")
        s_zt = sem("rows_transposed")
        s_ztc = sem("rows_transpose_copied")
        s_sc = sem("scores_ready")
        s_other = sem("other_nodes_marked")
        s_sm = sem("scores_masked")
        s_smt = sem("scores_transposed")
        s_cm = sem("column_maxima")
        s_bc = sem("maxima_spread")
        s_fold = sem("scores_folded")
        s_mn = sem("new_maxima")
        s_bt = sem("best_updated")
        s_df = sem("old_maxima_read")
        s_xe = sem("exponents_ready")
        s_e = sem("weights_ready")
        s_agg = sem("window_summed")
        s_kept = sem("sum_rescaled")
        s_acc = sem("sum_updated")
        s_one = sem("targets_marked")
        s_pre = sem("hidden_product")
        s_hid = sem("hidden_ready")
        s_cnt = sem("counts_updated")
        loop_sems = [s_base, *s_idx, *s_tgt, *s_ea, *s_win, s_turn, s_zt, s_ztc, s_sc, s_other, s_sm, s_smt,
                     s_cm, s_bc, s_fold, s_mn, s_bt, s_df, s_xe, s_e, s_agg, s_kept, s_acc, s_one, s_pre, s_hid, s_cnt]
        numbers = [s.num for s in loop_sems]
        assert numbers == list(range(numbers[0], numbers[0] + len(numbers)))
        loop_range = range(numbers[0], numbers[-1] + 1)

        src_g = src.rearrange("(g p j) -> g p j", p=P, j=J)
        dst_g = dst.rearrange("(g p j) -> g p j", p=P, j=J)
        ea_g = ea.rearrange("(g p j) d -> g p j d", p=P, j=J)

        def bases_of(eng, g, n):
            return nc.values_load_multi_w_load_instructions(
                base_i[0:1, bass.ds(g, n)], engines=[eng.engine], min_val=0, max_val=LAST_BASE)[1]

        def next_bases(dve):
            nc.vector.tensor_scalar(base_f[:, :], base_f[:, :], float(W), float(LAST_BASE), ALU.add,
                                    ALU.min).then_inc(s_base, 1)
            dve.wait_ge(s_base, 1)
            nc.vector.tensor_copy(base_i[:, :], base_f[:, :]).then_inc(s_base, 1)

        def load_group(sp, it, off, wait, window, query=False):
            s = slot(off)
            if wait:
                sp.wait_ge(s_agg, at(it, off) - RING + 1)
            g = at(it, off)
            sp.dma_start(idx[:, s, :], src_g[bass.ds(g, 1), :, :].rearrange("g p j -> p (g j)")).then_inc(s_idx[s], 16)
            sp.dma_start(tgt[:, s, :], dst_g[bass.ds(g, 1), :, :].rearrange("g p j -> p (g j)")).then_inc(s_tgt[s], 16)
            sp.dma_start(z[:, s, :, D:D + ED],
                         ea_g[bass.ds(g, 1), :, :, :].rearrange("g p j d -> p (g j) d")).then_inc(s_ea[s], 16)
            if query:
                sp.dma_start(Qw[:, s, :, :], query_cols[:, bass.ds(window, W), :]).then_inc(s_win[s], 16)
            else:
                sp.dma_start(Wg[D + ED:P, s, :], target_rows[bass.ds(window, W), :]).then_inc(s_win[s], 16)

        def gathered(r, it, off):
            a_round = STEPS + (1 if slot(off) < G - STEPS * RING else 0)
            return 16 * J * (uses(it, off) + 1) + r * (16 * J * a_round)

        def gather_group(pool, it, off, s_gath):
            s = slot(off)
            pool.wait_ge(s_idx[s], 16 * (uses(it, off) + 1))
            nc.gpsimd.sem_inc(s_turn, 1)
            for j in range(J):
                nc.gpsimd.indirect_dma_start(
                    z[:, s, j, 0:D], None, source_rows[:, :],
                    bass.IndirectOffsetOnAxis(ap=idx[:, s, j:j + 1].bitcast(U32), axis=0)).then_inc(s_gath[s], 16)

        def all_groups(eng, do):
            for off in range(RING):
                do(0, off, False)
            with eng.Fori(1, STEPS) as it:
                for off in range(RING):
                    do(it, off, True)
            for off in range(G - STEPS * RING):
                do(STEPS, off, True)

        def load_all(sp, query):
            b = bases_of(nc.sync, 0, RING)
            for off in range(RING):
                load_group(sp, 0, off, False, b[off], query)
            with nc.sync.Fori(1, STEPS) as it:
                b = bases_of(nc.sync, at(it, 0), RING)
                for off in range(RING):
                    load_group(sp, it, off, True, b[off], query)
            b = bases_of(nc.sync, at(STEPS, 0), G - STEPS * RING)
            for off in range(G - STEPS * RING):
                load_group(sp, STEPS, off, True, b[off], query)

        rounds = nc.values_load(rounds_i[0:1, 1:2], min_val=1, max_val=NP // W)
        with psum("p_zt", [P, 2, GE]) as p_zt, psum("p_s", [P, HEADS, 2, J, W]) as p_s, \
                psum("p_smt", [P, CHUNK]) as p_smt, psum("p_bc", [P, CHUNK]) as p_bc, \
                psum("p_agg", [P, CHUNK]) as p_agg, nc.Fori(0, rounds) as r:
            with nc.Block() as block:

                @block.sync
                def _(sp):
                    sp.wait_ge(s_base, 2)
                    load_all(sp, True)

                @block.gpsimd
                def _(pool):
                    all_groups(nc.gpsimd, lambda it, off, free: gather_group(pool, it, off, s_gath1))

                @block.tensor
                def _(pe):
                    def transpose_rows(it, off):
                        s, g = slot(off), at(it, off)
                        pe.wait_ge(s_gath1[s], gathered(r, it, off))
                        pe.wait_ge(s_ea[s], 16 * (uses(it, off) + 1))
                        if past(it, off, 2):
                            pe.wait_ge(s_ztc, g - 1)
                        for j in range(J):
                            last = nc.tensor.transpose(p_zt[0:P, off % 2, j * P:(j + 1) * P], z[:, s, j, :],
                                                       ident[:, :])
                        last.then_inc(s_zt, 1)

                    def scores(it, off, js):
                        if 0 in js:
                            pe.wait_ge(s_win[slot(off)], 16 * (uses(it, off) + 1))
                            pe.wait_ge(s_ztc, at(it, off) + 1)
                        for j in js:
                            last = nc.tensor.matmul(p_s[:, :, 0, j, :], zT[0:ZF, off % 2, j * P:(j + 1) * P],
                                                    Qw[:, slot(off), :, :].rearrange("p n h -> p h n"),
                                                    start=True, stop=True)
                        if J - 1 in js:
                            last.then_inc(s_sc, 1)

                    def scores_and_maxima(it, off):
                        scores(it, off, range(0, J // 2))
                        spread_maxima(it, off - 1)
                        scores(it, off, range(J // 2, J))

                    def turn_scores(it, off):
                        pe.wait_ge(s_fold, at(it, off) + 1)
                        nc.tensor.transpose(p_smt[:, 0:P], folded[:, off % 2, :], ident[:, :]).then_inc(s_smt, 1)

                    def spread_maxima(it, off):
                        pe.wait_ge(s_cm, at(it, off) + 1)
                        nc.tensor.matmul(p_bc[:, 0:HW], wide(colmax[:, off % 2:off % 2 + 1], [HW, P]),
                                         ident[0:HW, 0:HW], start=True, stop=True).then_inc(s_bc, 1)

                    def window_sums(it, off):
                        pe.wait_ge(s_e, at(it, off) + 1)
                        e = E[:, off % 2, 0:HEADS * J * W].rearrange("p (h j n) -> p h j n", h=HEADS, j=J)
                        for j in range(J):
                            last = nc.tensor.matmul(p_agg[0:ZF, 0:HW], z[:, slot(off), j, 0:ZF], e[:, :, j, :],
                                                    start=(j == 0), stop=(j == J - 1))
                        last.then_inc(s_agg, 1)

                    transpose_rows(0, 0)
                    scores(0, 0, range(J))
                    transpose_rows(0, 1)
                    turn_scores(0, 0)
                    scores_and_maxima(0, 1)
                    with nc.tensor.Fori(0, STEPS) as it:
                        for off in range(1, RING + 1):
                            transpose_rows(it, off + 1)
                            window_sums(it, off - 1)
                            turn_scores(it, off)
                            scores_and_maxima(it, off + 1)
                    window_sums(STEPS, 0)
                    turn_scores(STEPS, 1)
                    spread_maxima(STEPS, 1)
                    window_sums(STEPS, 1)

                @block.scalar
                def _(act):
                    def copy_rows(it, off):
                        act.wait_ge(s_zt, at(it, off) + 1)
                        if past(it, off, 2):
                            act.wait_ge(s_sc, at(it, off) - 1)
                        nc.scalar.copy(zT[0:ZF, off % 2, :], p_zt[0:ZF, off % 2, :]).then_inc(s_ztc, 1)

                    def weights(it, off):
                        act.wait_ge(s_xe, at(it, off) + 1)
                        nc.scalar.activation(E[:, off % 2, :], XE[:, off % 2, :], ACT.Exp).then_inc(s_e, 1)

                    copy_rows(0, 0)
                    copy_rows(0, 1)
                    with nc.scalar.Fori(0, STEPS) as it:
                        for off in range(1, RING + 1):
                            weights(it, off - 1)
                            copy_rows(it, off + 1)
                    weights(STEPS, 0)
                    weights(STEPS, 1)

                @block.vector
                def _(dve):
                    def mark_others(it, off, base):
                        s = slot(off)
                        dve.wait_ge(s_tgt[s], 16 * (uses(it, off) + 1))
                        nc.vector.tensor_tensor(
                            other[:, off % 2, :, :],
                            wide(node_id[:, bass.ds(base, W)].unsqueeze(1), [P, J, W]),
                            wide(tgt[:, s, :].unsqueeze(2), [P, J, W]), ALU.not_equal).then_inc(s_other, 1)

                    def mask_scores(it, off):
                        dve.wait_ge(s_other, at(it, off) + 1)
                        dve.wait_ge(s_sc, at(it, off) + 1)
                        nc.vector.scalar_tensor_tensor(
                            out=SM[:, off % 2, :, :, :].rearrange("p h j n -> p h (j n)"),
                            in0=wide(other[:, off % 2, :, :].rearrange("p j n -> p (j n)").unsqueeze(1),
                                     [P, HEADS, J * W]),
                            scalar=-FAR, in1=p_s[:, :, 0, :, :].rearrange("p h j n -> p h (j n)"),
                            op0=ALU.mult, op1=ALU.add).then_inc(s_sm, 1)
                        dve.wait_ge(s_sm, at(it, off) + 1)
                        nc.vector.tensor_reduce(folded[:, off % 2, 0:HW].rearrange("p (h n) -> p h n", h=HEADS),
                                                SM[:, off % 2, :, :, :].rearrange("p h j n -> p h n j"),
                                                AX.X, ALU.max).then_inc(s_fold, 1)

                    def column_maxima(it, off):
                        dve.wait_ge(s_smt, at(it, off) + 1)
                        nc.vector.tensor_reduce(colmax[:, off % 2:off % 2 + 1], p_smt[0:HW, 0:P], AX.X,
                                                ALU.max).then_inc(s_cm, 1)

                    def new_maxima(it, off, base):
                        g = at(it, off)
                        old = best[:, :, bass.ds(base, W)]
                        now = p_bc[:, 0:HW].rearrange("p (h n) -> p h n", h=HEADS)
                        xe = XE[:, off % 2, :]
                        dve.wait_ge(s_bc, g + 1)
                        if past(it, off, 1):
                            dve.wait_ge(s_bt, g)
                        nc.vector.tensor_tensor(mnew[:, :, :], old, now, ALU.max).then_inc(s_mn, 1)
                        dve.wait_ge(s_mn, g + 1)
                        nc.vector.tensor_tensor(
                            xe[:, HEADS * J * W:].rearrange("p (h n) -> p h n", h=HEADS), old, mnew[:, :, :],
                            ALU.subtract).then_inc(s_df, 1)
                        nc.vector.tensor_tensor(
                            xe[:, 0:HEADS * J * W].rearrange("p (h j n) -> p h j n", h=HEADS, j=J),
                            SM[:, off % 2, :, :, :], wide(mnew[:, :, :].unsqueeze(2), [P, HEADS, J, W]),
                            ALU.subtract).then_inc(s_xe, 1)
                        dve.wait_ge(s_df, g + 1)
                        nc.vector.tensor_tensor(old, old, mnew[:, :, :], ALU.max).then_inc(s_bt, 1)

                    def add_sums(it, off, base):
                        g = at(it, off)
                        a = acc[0:ZF, :, bass.ds(base, W)]
                        dve.wait_ge(s_agg, g + 1)
                        if past(it, off, 1):
                            dve.wait_ge(s_acc, g)
                        nc.vector.tensor_tensor(
                            kept[0:ZF, :, :], a,
                            E[0:ZF, off % 2, HEADS * J * W:].rearrange("p (h n) -> p h n", h=HEADS),
                            ALU.mult).then_inc(s_kept, 1)
                        dve.wait_ge(s_kept, g + 1)
                        nc.vector.tensor_tensor(
                            a, kept[0:ZF, :, :], p_agg[0:ZF, 0:HW].rearrange("p (h n) -> p h n", h=HEADS),
                            ALU.add).then_inc(s_acc, 1)

                    def turn(it, off, b, last=False):
                        mask_scores(it, off)
                        b += bases_of(nc.vector, at(it, off - 1 + len(b)), (2 if last else 3) - len(b))
                        column_maxima(it, off)
                        add_sums(it, off - 1, b[0])
                        if not last:
                            mark_others(it, off + 1, b[2])
                        new_maxima(it, off, b[1])
                        return b[1:]

                    next_bases(dve)
                    dve.wait_ge(s_base, 2)
                    b = bases_of(nc.vector, 0, 2)
                    mark_others(0, 0, b[0])
                    mask_scores(0, 0)
                    column_maxima(0, 0)
                    mark_others(0, 1, b[1])
                    new_maxima(0, 0, b[0])
                    for off in range(1, RING + 1):
                        b = turn(0, off, b)
                    with nc.vector.Fori(1, STEPS) as it:
                        b = []
                        for off in range(1, RING + 1):
                            b = turn(it, off, b)
                    b = turn(STEPS, 1, [], last=True)
                    add_sums(STEPS, 1, b[0])

            nc.all_engine_barrier(sems_to_clear=loop_range)

        s_o = sem("heads_product")
        s_oc = sem("heads_copied")
        s_o2 = sem("attention_normalized")
        s_m1 = sem("mlp_first")
        s_m1c = sem("mlp_gelu")
        s_m2 = sem("mlp_second")
        s_m2c = sem("mlp_added")
        s_x1 = sem("first_layer_out")
        s_r = sem("target_product")
        s_rc = sem("target_copied")
        s_tab2 = sem("second_tables_out")
        s_c = sem("message_weights_in")
        T3 = 3
        OG = [(t, min(t + T3, NT)) for t in range(0, NT, T3)]
        with psum("p_o", [P, 2, CHUNK]) as p_o, psum("p_t", [D, 2, CHUNK]) as p_t, psum("p_m", [D, 2, CHUNK]) as p_m, \
                psum("p_n", [P, 2, CHUNK]) as p_n, nc.Block() as block:

            @block.tensor
            def _(pe):
                for n, (a, b) in enumerate(OG):
                    if n >= 2:
                        pe.wait_ge(s_oc, n - 1)
                    for t in range(a, b):
                        for h in range(HEADS):
                            c = ((t - a) * HEADS + h) * (D + 1)
                            last = nc.tensor.matmul(p_o[:, n % 2, c:c + D + 1], acc[0:ZF, h, t * P:(t + 1) * P],
                                                    U[:, h, :], start=True, stop=True)
                    last.then_inc(s_o, 1)

                def turn_nodes(n, a, b, of, ready):
                    pe.wait_ge(ready, 1)
                    for t in range(a // P, b // P):
                        last = nc.tensor.transpose(p_t[:, n % 2, t * P - a:t * P - a + P], of[:, t, :], ident[:, :])
                    last.then_inc(s_tp, 1)

                for n, (a, b) in enumerate(CHUNKS):
                    if n >= 2:
                        pe.wait_ge(s_tc, len(CHUNKS) + n - 1)
                    turn_nodes(n, a, b, H, s_o2)
                    pe.wait_ge(s_tc, len(CHUNKS) + n + 1)
                    nc.tensor.matmul(p_m[:, n % 2, 0:b - a], W1B[:, :], nodesT[:, a:b], start=True,
                                     stop=True).then_inc(s_m1, 1)
                    pe.wait_ge(s_m1c, n + 1)
                    if n >= 2:
                        pe.wait_ge(s_m2c, n - 1)
                    for t in range(a // P, b // P):
                        last = nc.tensor.matmul(p_n[:, n % 2, t * D - a * D // P:(t + 1) * D - a * D // P],
                                                nodesT2[:, t * P:(t + 1) * P], W2B[:, :], start=True, stop=True)
                    last.then_inc(s_m2, 1)
                for n, (a, b) in enumerate(CHUNKS):
                    if n >= 2:
                        pe.wait_ge(s_tc, 2 * len(CHUNKS) + n - 1)
                    turn_nodes(n, a, b, X, s_x1)
                    pe.wait_ge(s_tc, 2 * len(CHUNKS) + n + 1)
                    if n >= 2:
                        pe.wait_ge(s_rc, n - 1)
                    for t in range(a // P, b // P):
                        last = nc.tensor.matmul(p_n[:, n % 2, t * P - a:(t + 1) * P - a], nodesT[:, t * P:(t + 1) * P],
                                                mWB[:, :], start=True, stop=True)
                    last.then_inc(s_r, 1)

            @block.scalar
            def _(act):
                for n, (a, b) in enumerate(OG):
                    act.wait_ge(s_o, n + 1)
                    w = (b - a) * HEADS * (D + 1)
                    nc.scalar.copy(heads_out[:, a:b, :, :].rearrange("p t h d -> p (t h d)"),
                                   p_o[:, n % 2, 0:w]).then_inc(s_oc, 1)
                deviation(act, 2)
                for n, (a, b) in enumerate(CHUNKS):
                    act.wait_ge(s_tp, len(CHUNKS) + n + 1)
                    nc.scalar.copy(nodesT[0:D, a:b], p_t[:, n % 2, 0:b - a]).then_inc(s_tc, 1)
                    act.wait_ge(s_m1, n + 1)
                    nc.scalar.activation(nodesT2[0:D, a:b], p_m[:, n % 2, 0:b - a], ACT.Gelu).then_inc(s_m1c, 1)
                deviation(act, 3)
                for n, (a, b) in enumerate(CHUNKS):
                    act.wait_ge(s_tp, 2 * len(CHUNKS) + n + 1)
                    nc.scalar.copy(nodesT[0:D, a:b], p_t[:, n % 2, 0:b - a]).then_inc(s_tc, 1)

            @block.vector
            def _(dve):
                dve.wait_ge(s_oc, len(OG))
                den = heads_out[:, :, :, D:D + 1]
                num = heads_out[:, :, :, 0:D]
                link(dve, nc.vector.tensor_scalar(den, den, 1e-8, None, ALU.add))
                link(dve, nc.vector.reciprocal(den, den))
                link(dve, nc.vector.tensor_tensor(num, num, wide(den, [P, NT, HEADS, D]), ALU.mult))
                link(dve, nc.vector.tensor_tensor(T[:, :, :], num[:, :, 0, :], num[:, :, 1, :], ALU.add))
                link(dve, nc.vector.tensor_tensor(RES[:, :, :], T[:, :, :], X[:, :, :], ALU.add))
                link(dve, nc.vector.tensor_tensor(RES[:, :, :], RES[:, :, :], wide(rows[:, 4:5, :], [P, NT, D]),
                                                  ALU.add))
                link(dve, normalize(dve, RES[:, :, :], H[:, :, :], T[:, :, :], 2))
                scale_shift(dve, H[:, :, :], 2).then_inc(s_o2, 1)
                link(dve, nc.vector.tensor_tensor(RES[:, :, :], RES[:, :, :], X[:, :, :], ALU.add))
                for n, (a, b) in enumerate(CHUNKS):
                    dve.wait_ge(s_m2, n + 1)
                    res = RES[:, a // P:b // P, :]
                    nc.vector.tensor_tensor(res, res, p_n[:, n % 2, 0:(b - a) // P * D].rearrange("p (t d) -> p t d", d=D),
                                            ALU.add).then_inc(s_m2c, 1)
                dve.wait_ge(s_m2c, len(CHUNKS))
                normalize(dve, RES[:, :, :], X[:, :, :], T[:, :, :], 3).then_inc(s_x1, 1)
                for n, (a, b) in enumerate(CHUNKS):
                    dve.wait_ge(s_r, n + 1)
                    nc.vector.tensor_copy(R_out[:, a // P:b // P, :].rearrange("p t n -> p (t n)"),
                                          p_n[:, n % 2, 0:b - a]).then_inc(s_rc, 1)
                nc.vector.memset(queryT[:, :, :], 0.0)
                nc.vector.memset(cnt[:, :], 0.0)
                nc.vector.tensor_scalar(base_f[:, :], base0[:, 0, :], float(-W), None, ALU.add)

            @block.sync
            def _(sp):
                for i in range(RING):
                    sp.dma_start(Wg[0:D, i, :], mW1[0:D, :]).then_inc(s_c, 16)
                    sp.dma_start(Wg[D:D + ED, i, :], mW1[2 * D:2 * D + ED, :]).then_inc(s_c, 16)
                sp.wait_ge(s_x1, 1)
                sp.dma_start(source_rows.rearrange("(t p) d -> p t d", p=P), X[:, :, :]).then_inc(s_tab2, 16)
                sp.wait_ge(s_rc, len(CHUNKS))
                sp.dma_start(target_rows.rearrange("(t p) d -> p t d", p=P), R_out).then_inc(s_tab2, 16)
                sp.wait_ge(s_c, 32 * RING)
                sp.wait_ge(s_tab2, 32)

        rounds2 = nc.values_load(rounds_i[0:1, 1:2], min_val=1, max_val=NP // W)
        with psum("p_zt2", [P, 2, GE]) as p_zt, psum("p_pre", [P, 2, J * HID]) as p_pre, \
                psum("p_sum", [P, 2, CHUNK]) as p_sum, psum("p_cnt", [P, 2, CHUNK]) as p_cnt, nc.Fori(0, rounds2) as r:
            with nc.Block() as block:

                @block.sync
                def _(sp):
                    sp.wait_ge(s_base, 2)
                    load_all(sp, False)

                @block.gpsimd
                def _(pool):
                    all_groups(nc.gpsimd, lambda it, off, free: gather_group(pool, it, off, s_gath2))

                @block.tensor
                def _(pe):
                    def transpose_rows(it, off):
                        s, g = slot(off), at(it, off)
                        pe.wait_ge(s_gath2[s], gathered(r, it, off))
                        pe.wait_ge(s_ea[s], 16 * (uses(it, off) + 1))
                        pe.wait_ge(s_one, g + 1)
                        if past(it, off, 2):
                            pe.wait_ge(s_ztc, g - 1)
                        for j in range(J):
                            last = nc.tensor.transpose(p_zt[:, off % 2, j * P:(j + 1) * P], z[:, s, j, :],
                                                       ident[:, :])
                        last.then_inc(s_zt, 1)

                    def hidden(it, off):
                        pe.wait_ge(s_ztc, at(it, off) + 1)
                        pe.wait_ge(s_win[slot(off)], 16 * (uses(it, off) + 1))
                        for j in range(J):
                            last = nc.tensor.matmul(p_pre[:, off % 2, j * HID:(j + 1) * HID],
                                                    zT[:, off % 2, j * P:(j + 1) * P], Wg[:, slot(off), :],
                                                    start=True, stop=True)
                        last.then_inc(s_pre, 1)

                    def window_sums(it, off):
                        g = at(it, off)
                        pe.wait_ge(s_hid, g + 1)
                        if past(it, off, 2):
                            pe.wait_ge(s_acc, g - 1)
                        mark = z[:, slot(off), :, D + ED:P]
                        for j in range(J):
                            nc.tensor.matmul(p_cnt[0:1, off % 2, 0:W], ones[:, :], mark[:, j, :],
                                             start=(j == 0), stop=(j == J - 1))
                        for j in range(J):
                            last = nc.tensor.matmul(p_sum[:, off % 2, 0:W], hid[:, off % 2, j, :], mark[:, j, :],
                                                    start=(j == 0), stop=(j == J - 1))
                        last.then_inc(s_agg, 1)

                    transpose_rows(0, 0)
                    transpose_rows(0, 1)
                    hidden(0, 0)
                    for off in range(1, RING + 1):
                        transpose_rows(0, off + 1)
                        hidden(0, off)
                        window_sums(0, off - 1)
                    with nc.tensor.Fori(1, STEPS) as it:
                        for off in range(1, RING + 1):
                            transpose_rows(it, off + 1)
                            hidden(it, off)
                            window_sums(it, off - 1)
                    hidden(STEPS, 1)
                    window_sums(STEPS, 0)
                    window_sums(STEPS, 1)

                @block.scalar
                def _(act):
                    def hidden_relu(it, off):
                        act.wait_ge(s_pre, at(it, off) + 1)
                        nc.scalar.activation(hid[:, off % 2, :, :].rearrange("p j n -> p (j n)"),
                                             p_pre[:, off % 2, :], ACT.Relu).then_inc(s_hid, 1)

                    hidden_relu(0, 0)
                    with nc.scalar.Fori(0, STEPS) as it:
                        for off in range(1, RING + 1):
                            hidden_relu(it, off)
                    hidden_relu(STEPS, 1)

                @block.vector
                def _(dve):
                    def mark_targets(it, off, base):
                        s = slot(off)
                        dve.wait_ge(s_tgt[s], 16 * (uses(it, off) + 1))
                        nc.vector.tensor_tensor(
                            z[:, s, :, D + ED:P], wide(node_id[:, bass.ds(base, W)].unsqueeze(1), [P, J, W]),
                            wide(tgt[:, s, :].unsqueeze(2), [P, J, W]), ALU.is_equal).then_inc(s_one, 1)

                    def copy_rows(it, off):
                        dve.wait_ge(s_zt, at(it, off) + 1)
                        if past(it, off, 2):
                            dve.wait_ge(s_pre, at(it, off) - 1)
                        nc.vector.tensor_copy(zT[:, off % 2, :], p_zt[:, off % 2, :]).then_inc(s_ztc, 1)

                    def add_sums(it, off, base):
                        g = at(it, off)
                        a, c = msgT[:, bass.ds(base, W)], cnt[:, bass.ds(base, W)]
                        dve.wait_ge(s_agg, g + 1)
                        if past(it, off, 1):
                            dve.wait_ge(s_acc, g)
                        nc.vector.tensor_tensor(c, c, p_cnt[0:1, off % 2, 0:W], ALU.add)
                        nc.vector.tensor_tensor(a, a, p_sum[:, off % 2, 0:W], ALU.add).then_inc(s_acc, 1)

                    def turn(it, off, b):
                        copy_rows(it, off + 1)
                        add_sums(it, off - 1, b[0])
                        mark_targets(it, off + 2, b[3])

                    next_bases(dve)
                    dve.wait_ge(s_base, 2)
                    b = bases_of(nc.vector, 0, 3)
                    for off in range(3):
                        mark_targets(0, off, b[off])
                    copy_rows(0, 0)
                    copy_rows(0, 1)
                    for off in range(1, RING + 1):
                        b = bases_of(nc.vector, off - 1, 4)
                        turn(0, off, b)
                    with nc.vector.Fori(1, STEPS - 1) as it:
                        b = bases_of(nc.vector, at(it, 0), RING + 3)
                        for off in range(1, RING + 1):
                            turn(it, off, b[off - 1:off + 3])
                    for off in range(1, RING):
                        b = bases_of(nc.vector, at(STEPS - 1, off - 1), 4)
                        turn(STEPS - 1, off, b)
                    b = bases_of(nc.vector, at(STEPS, -1), 3)
                    copy_rows(STEPS, 1)
                    add_sums(STEPS - 1, RING - 1, b[0])
                    add_sums(STEPS, 0, b[1])
                    add_sums(STEPS, 1, b[2])

            nc.all_engine_barrier(sems_to_clear=loop_range)

        s_g = sem("messages_product")
        s_gc = sem("messages_copied")
        s_u1 = sem("update_first")
        s_u1c = sem("update_relu")
        s_u2 = sem("update_second")
        s_u2c = sem("update_added")
        s_y = sem("output_ready")
        s_out = sem("output_written")
        with psum("p_g", [D, 2, CHUNK]) as p_g, psum("p_u", [P, 2, CHUNK]) as p_u, psum("p_v", [P, 2, CHUNK]) as p_v, \
                nc.Block() as block:

            @block.tensor
            def _(pe):
                for n, (a, b) in enumerate(CHUNKS):
                    nc.tensor.matmul(p_g[:, n % 2, 0:b - a], mW2S[:, :], msgT[:, a:b], start=True, stop=False)
                    nc.tensor.matmul(p_g[:, n % 2, 0:b - a], mb2S[:, :], cnt[:, a:b], start=False,
                                     stop=True).then_inc(s_g, 1)
                    if n >= 2:
                        pe.wait_ge(s_u1c, n - 1)
                    nc.tensor.matmul(p_u[:, n % 2, 0:b - a], uWA[:, :], nodesT[:, a:b], start=True, stop=False)
                    pe.wait_ge(s_gc, n + 1)
                    nc.tensor.matmul(p_u[:, n % 2, 0:b - a], uWB[:, :], nodesT2[0:D, a:b], start=False,
                                     stop=True).then_inc(s_u1, 1)
                    pe.wait_ge(s_u1c, n + 1)
                    if n >= 2:
                        pe.wait_ge(s_u2c, n - 1)
                    for t in range(a // P, b // P):
                        c = (t * P - a) * D // P
                        last = nc.tensor.matmul(p_v[:, n % 2, c:c + D], hidT[:, t * P:(t + 1) * P], uW2S[:, :],
                                                start=True, stop=True)
                    last.then_inc(s_u2, 1)

            @block.scalar
            def _(act):
                for n, (a, b) in enumerate(CHUNKS):
                    act.wait_ge(s_g, n + 1)
                    nc.scalar.copy(nodesT2[0:D, a:b], p_g[:, n % 2, 0:b - a]).then_inc(s_gc, 1)
                    act.wait_ge(s_u1, n + 1)
                    nc.scalar.activation(hidT[:, a:b], p_u[:, n % 2, 0:b - a], ACT.Relu).then_inc(s_u1c, 1)
                deviation(act, 4)

            @block.vector
            def _(dve):
                link(dve, nc.vector.tensor_tensor(RES[:, :, :], X[:, :, :], wide(rows[:, 5:6, :], [P, NT, D]), ALU.add))
                for n, (a, b) in enumerate(CHUNKS):
                    dve.wait_ge(s_u2, n + 1)
                    res = RES[:, a // P:b // P, :]
                    nc.vector.tensor_tensor(res, res, p_v[:, n % 2, 0:(b - a) // P * D].rearrange("p (t d) -> p t d", d=D),
                                            ALU.add).then_inc(s_u2c, 1)
                dve.wait_ge(s_u2c, len(CHUNKS))
                normalize(dve, RES[:, :, :], H[:, :, :], T[:, :, :], 4).then_inc(s_y, 1)

            @block.sync
            def _(sp):
                sp.wait_ge(s_y, 1)
                sp.dma_start(out[0:FULL_T * P, :].rearrange("(t p) d -> p t d", p=P), H[:, 0:FULL_T, :]).then_inc(s_out, 16)
                sp.dma_start(out[FULL_T * P:NODES, :], H[0:LAST_N, FULL_T, :]).then_inc(s_out, 16)
                sp.wait_ge(s_out, 32)


WEIGHT_LOADS = 2 + 6 + 1 + 8 + 4 + 6

_INS = ['x', 'src', 'dst', 'edge_attr_32'] + ['L0_gnn_' + k for k in (
    'Wq bq Wk bk Wv bv We Wp bp ln1_g ln1_b ln2_g ln2_b W1 b1 W2 b2').split()] + ['L1_gnn_' + k for k in (
    'mW1 mb1 mW2 mb2 uW1 ub1 uW2 ub2').split()]
_PAD = {'src': 0, 'dst': NO_NODE, 'edge_attr_32': 0}


def kernel(**inputs):
    import numpy as _np
    import concourse.bacc as _bacc
    from concourse import mybir as _mybir
    from concourse.bass_utils import run_bass_kernel_spmd as _run

    nc = _bacc.Bacc("TRN2", target_bir_lowering=False, num_devices=1)
    arrays, args = {}, []
    for name in _INS:
        a = _np.ascontiguousarray(inputs[name])
        if name in _PAD:
            a = _np.concatenate([a, _np.full((EP - EDGES,) + a.shape[1:], _PAD[name], a.dtype)])
        arrays[f"in_{name}_dram"] = a
        args.append(nc.dram_tensor(f"in_{name}_dram", a.shape, _mybir.dt.from_np(a.dtype), kind="ExternalInput").ap())
    args.append(nc.dram_tensor("out_0_dram", (NODES, D), F32, kind="ExternalOutput").ap())
    build(nc, *args)
    r = _run(nc, [arrays], core_ids=[0])
    return r.results[0]["out_0_dram"]
```

```python
from contextlib import ExitStack

import concourse.bass as bass
from concourse import mybir

F32 = mybir.dt.float32
I32 = mybir.dt.int32
U32 = mybir.dt.uint32
ALU = mybir.AluOpType
ACT = mybir.ActivationFunctionType
AX = mybir.AxisListType

P = 128
NODES = 3125
EDGES = 103125
D = 64
ED = 32
HEADS = 2
HC = HEADS * D
HID = 128
EPS = 1e-5

NT = -(-NODES // P)
FULL_T = NODES // P
LAST_N = NODES - FULL_T * P
NP = NT * P
CHUNK = 512
PART = 12
A, B = slice(0, PART), slice(PART, NT)
CHUNKS = [(c, min(c + CHUNK, NP)) for c in range(0, NP, CHUNK)]

J = 4
GE = P * J
G = -(-EDGES // GE)
EP = G * GE
W = 32
NO_NODE = 1 << 20
LAST_BASE = NP - W
assert LAST_BASE >= NODES
HW = HEADS * W

RING = 8
STEPS = (G - 2) // RING
assert G == STEPS * RING + 2 and RING % 2 == 0

ZF = D + ED + 1
FAR = 1e30
NO_MAX = -1e20


def slot(off):
    return off % RING


def uses(it, off):
    return it + off // RING


def at(it, off):
    return it * RING + off


def past(it, off, n):
    return not isinstance(it, int) or at(it, off) >= n


def build(nc, x, src, dst, ea, Wq, bq, Wk, bk, Wv, bv, We, Wp, bp, ln1_g, ln1_b, ln2_g, ln2_b, W1, b1, W2, b2,
          mW1, mb1, mW2, mb2, uW1, ub1, uW2, ub2, out):
    with ExitStack() as ctx:
        def sb(name, shape, dt=F32):
            return ctx.enter_context(nc.sbuf_tensor(name, shape, dt))

        def sem(name):
            return ctx.enter_context(nc.semaphore(name))

        source_rows = nc.dram_tensor("source_rows", (NP, D), F32).ap()
        query_cols = nc.dram_tensor("query_cols", (ZF, NP, HEADS), F32).ap()
        target_rows = nc.dram_tensor("target_rows", (NP, HID), F32).ap()
        lohi_dram = nc.dram_tensor("lohi_dram", (2, G), F32).ap()

        ident = sb("ident", [P, P])
        ones = sb("ones", [P, 1])
        node_id = sb("node_id", [P, NP])
        X = sb("X", [P, NT, D])
        H = sb("H", [P, NT, D])
        T = sb("T", [P, NT, D])
        RES = sb("RES", [P, NT, D])
        stat = sb("stat", [P, 4, NT])
        rows = sb("rows", [P, 6, D])
        nodesT = sb("nodesT", [D + 2, NP])
        nodesT2 = sb("nodesT2", [D + 1, NP])
        queryT = sb("queryT", [P, NP, HEADS])
        best = sb("best", [P, HEADS, NP])
        acc = sb("acc", [P, HEADS, NP])
        base0 = sb("base0", [1, 2, G])
        base_f = sb("base_f", [1, G])
        base_i = sb("base_i", [1, G], I32)
        lohi_sb = sb("lohi_sb", [G // 2, 2, 2])
        span = sb("span", [1, 2])
        rounds_i = sb("rounds_i", [1, 2], I32)
        WqB = sb("WqB", [D + 1, HC])
        Wkc = sb("Wkc", [ZF, HC])
        Wvc = sb("Wvc", [ZF, HC])
        WkcT = sb("WkcT", [P, ZF])
        WvcT = sb("WvcT", [P, ZF])
        WpS = sb("WpS", [P, D])
        U = sb("U", [ZF, HEADS, D + 1])
        W1B = sb("W1B", [D + 1, D])
        W2B = sb("W2B", [D + 1, D])
        mWB = sb("mWB", [D + 1, HID])
        mW2S = sb("mW2S", [P, D])
        mW2T = sb("mW2T", [D, HID])
        mb2S = sb("mb2S", [D, 1])
        msgW = sb("msgW", [HID, HID])
        cntW = sb("cntW", [1, HID])
        uWA = sb("uWA", [D + 2, HID])
        WqT = sb("WqT", [P, D + 1])
        queryW = sb("queryW", [D + 1, HEADS, ZF])
        uWB = sb("uWB", [D, HID])
        uW2S = sb("uW2S", [P, D])
        idx = sb("idx", [P, RING, J], I32)
        tgt = sb("tgt", [P, RING, J], I32)
        z = sb("z", [P, RING, J, P])
        zT = sb("zT", [P, 2, GE])
        other = sb("other", [P, 2, J, W])
        SM = sb("SM", [P, 2, HEADS, J, W])
        folded = sb("folded", [P, 2, P])
        Qw = sb("Qw", [ZF, RING, W, HEADS])
        colmax = sb("colmax", [P, 2])
        mnew = sb("mnew", [P, HEADS, W])
        XE = sb("XE", [P, 2, HEADS * J * W + HW])
        E = sb("E", [P, 2, HEADS * J * W + HW])
        kept = sb("kept", [P, HEADS, W])
        Wg = sb("Wg", [P, RING, HID])
        hid = sb("hid", [P, 2, J, HID])
        cnt = sb("cnt", [1, NP])

        heads_out = best[:, :, :].rearrange("p h n -> p (h n)")[:, 0:NT * HEADS * D].rearrange(
            "p (t h d) -> p t h d", t=NT, h=HEADS)
        heads_den = T[:, :, 0:HEADS]
        dst_rows = RES[:, :, :].rearrange("p t d -> p (t d)")[0:G // 2, 0:2 * GE].bitcast(I32).rearrange(
            "p (a e) -> p a e", a=2)
        dst_real = hid[:, :, :, :].rearrange("p a j n -> p (a j n)")[0:G // 2, :].rearrange("p (a e) -> p a e", a=2)
        lohi = lohi_sb[:, :, :]
        R_out = acc[:, 0, :].rearrange("p (t n) -> p t n", t=NT)
        queryT_flat = queryT[:, :, :].rearrange("p n h -> p (n h)")
        msgT = queryT_flat[:, 0:NP]
        hidT = queryT_flat[:, NP:]

        def psum(name, shape):
            return nc.psum_tensor(name, shape, F32)

        def wide(row, shape):
            return row.broadcast_to(shape)

        s_w = sem("weights_in")
        s_late = sem("later_weights_in")
        s_wp = sem("weight_products_copied")
        s_x = sem("x_in")
        s_x2 = sem("x_second_part_in")
        s_xpad = sem("x_padding_zeroed")
        s_onerow = sem("ones_rows_set")
        s_ident0 = sem("ident_cleared")
        s_ident = sem("ident_ready")
        s_dve = sem("vector_step")
        s_pool = sem("gpsimd_step")
        s_var = sem("variance_ready")
        s_std = sem("deviation_ready")
        s_h = sem("normalized_ready")
        s_tp = sem("transposed")
        s_tc = sem("transpose_copied")
        s_qq = sem("score_product")
        s_qqc = sem("score_copied")
        s_wt = sem("weights_transposed")
        s_wtc = sem("weights_transpose_copied")
        s_dst = sem("dst_rows_in")
        s_lohi = sem("lohi_ready")
        s_lod = sem("lohi_out")
        s_lor = sem("lohi_row_in")
        s_tab = sem("source_rows_out")

        steps = [0]

        def link(eng, ins):
            steps[0] += 1
            ins.then_inc(s_dve, 1)
            eng.wait_ge(s_dve, steps[0])

        def normalize(dve, a, b, scratch, turn, part):
            a, b, scratch = a[:, part, :], b[:, part, :], scratch[:, part, :]
            mean, rstd, var, dev = (stat[:, k, part] for k in range(4))
            tiles = part.stop - part.start
            link(dve, nc.vector.tensor_reduce(mean, a, AX.X, ALU.add))
            link(dve, nc.vector.tensor_scalar(mean, mean, 1.0 / D, None, ALU.mult))
            link(dve, nc.vector.tensor_tensor(b, a, wide(mean.unsqueeze(2), [P, tiles, D]), ALU.subtract))
            link(dve, nc.vector.tensor_tensor(scratch, b, b, ALU.mult))
            link(dve, nc.vector.tensor_reduce(rstd, scratch, AX.X, ALU.add))
            nc.vector.tensor_scalar(var, rstd, 1.0 / D, EPS, ALU.mult, ALU.add).then_inc(s_var, 1)
            dve.wait_ge(s_std, turn)
            link(dve, nc.vector.reciprocal(rstd, dev))
            return nc.vector.tensor_tensor(b, b, wide(rstd.unsqueeze(2), [P, tiles, D]), ALU.mult)

        def deviation(act, turn, part):
            act.wait_ge(s_var, turn)
            nc.scalar.activation(stat[:, 3, part], stat[:, 2, part], ACT.Sqrt).then_inc(s_std, 1)

        def scale_shift(dve, a, k, part):
            a = a[:, part, :]
            shape = [P, part.stop - part.start, D]
            link(dve, nc.vector.tensor_tensor(a, a, wide(rows[:, k:k + 1, :], shape), ALU.mult))
            return nc.vector.tensor_tensor(a, a, wide(rows[:, k + 1:k + 2, :], shape), ALU.add)

        def line(v):
            return v.rearrange("(a n) -> a n", a=1)

        def spread(row):
            return row.rearrange("(a d) -> a d", a=1).partition_broadcast(P)

        early_loads = [(rows[:, 0, :], spread(ln1_g)), (rows[:, 1, :], spread(ln1_b)),
                       (WqB[0:D, :], Wq), (WqB[D:D + 1, :], line(bq)),
                       (Wkc[0:D, :], Wk), (Wkc[D:D + ED, :], We), (Wkc[D + ED:ZF, :], line(bk)),
                       (Wvc[0:D, :], Wv), (Wvc[D:D + ED, :], We), (Wvc[D + ED:ZF, :], line(bv)),
                       (WpS[:, :], Wp), (mW2S[:, :], mW2), (uWB[:, :], uW1[D:2 * D, :]),
                       (mb2S[:, :], mb2.rearrange("(n a) -> n a", a=1))]
        late_loads = [(W1B[0:D, :], W1), (W1B[D:D + 1, :], line(b1)), (W2B[0:D, :], W2), (W2B[D:D + 1, :], line(b2)),
                      (mWB[0:D, :], mW1[D:2 * D, :]), (mWB[D:D + 1, :], line(mb1)),
                      (uWA[0:D, :], uW1[0:D, :]), (uWA[D:D + 1, :], line(ub1)), (uW2S[:, :], uW2)]
        late_loads += [(rows[:, k, :], spread(r)) for k, r in ((2, ln2_g), (3, ln2_b), (4, bp), (5, ub2))]

        with psum("pT", [D, 2, CHUNK]) as pT, psum("pW", [P, 2, CHUNK]) as pW, \
                psum("pS", [P, 2, 2, CHUNK]) as pS, nc.Block() as block:

            @block.sync
            def _(sp):
                sp.dma_start(X[:, 0:PART, :], x[0:PART * P, :].rearrange("(t p) d -> p t d", p=P)).then_inc(s_x, 16)
                sp.dma_start(X[:, PART:FULL_T, :],
                             x[PART * P:FULL_T * P, :].rearrange("(t p) d -> p t d", p=P)).then_inc(s_x2, 16)
                sp.wait_ge(s_xpad, 1)
                sp.dma_start(X[0:LAST_N, FULL_T, :], x[FULL_T * P:NODES, :]).then_inc(s_x2, 16)
                sp.dma_start(dst_rows, dst.rearrange("(p a e) -> p a e", a=2, e=GE)).then_inc(s_dst, 16)
                sp.wait_ge(s_lohi, 1)
                for k in range(2):
                    sp.dma_start(lohi_dram[k, :].rearrange("(p a) -> p a", a=2), lohi[:, k, :]).then_inc(s_lod, 16)
                sp.wait_ge(s_lod, 32)
                sp.dma_start(base0[:, :, :], lohi_dram.rearrange("(o k) g -> o k g", o=1)).then_inc(s_lor, 16)
                sp.wait_ge(s_h, 2)
                sp.dma_start(source_rows.rearrange("(t p) d -> p t d", p=P), H[:, :, :]).then_inc(s_tab, 16)
                sp.wait_ge(s_wp, 2)
                sp.dma_start(uWA[D + 1:D + 2, :], cntW[:, :]).then_inc(s_tab, 16)
                for n, (a, b) in enumerate(CHUNKS):
                    sp.wait_ge(s_qqc, n + 1)
                    sp.dma_start(query_cols[:, a:b, :], queryT[0:ZF, a:b, :]).then_inc(s_tab, 16)
                sp.wait_ge(s_late, 16 * len(late_loads))
                sp.wait_ge(s_tab, 16 * (2 + len(CHUNKS)))

            @block.gpsimd
            def _(pool):
                nc.gpsimd.memset(ident[:, :], 0.0).then_inc(s_ident0, 1)
                pool.wait_ge(s_ident0, 1)
                nc.gpsimd.affine_select(out=ident[:, :], in_=ident[:, :], compare_op=ALU.not_equal, fill=1.0, base=0,
                                        pattern=[[-1, P]], channel_multiplier=1).then_inc(s_ident, 1)
                pool.wait_ge(s_ident, 1)
                nc.gpsimd.memset(nodesT[D:D + 1, :], 1.0).then_inc(s_onerow, 1)
                pool.wait_ge(s_onerow, 1)
                nc.gpsimd.iota(node_id[:, :], [[1, NP]], base=0, channel_multiplier=0,
                               allow_small_or_imprecise_dtypes=True).then_inc(s_pool, 1)
                pool.wait_ge(s_pool, 1)
                nc.gpsimd.memset(z[:, :, :, D + ED:P], 1.0).then_inc(s_pool, 1)
                pool.wait_ge(s_pool, 2)
                nc.gpsimd.memset(folded[:, :, :], 0.0).then_inc(s_pool, 1)
                pool.wait_ge(s_pool, 3)
                nc.gpsimd.memset(best[:, :, :], NO_MAX).then_inc(s_pool, 1)
                pool.wait_ge(s_pool, 4)
                nc.gpsimd.memset(acc[:, :, :], 0.0).then_inc(s_pool, 1)
                pool.wait_ge(s_pool, 5)
                nc.gpsimd.memset(nodesT2[D:D + 1, :], 1.0).then_inc(s_pool, 1)
                pool.wait_ge(s_pool, 6)
                nc.gpsimd.memset(ones[:, :], 1.0).then_inc(s_pool, 1)
                pool.wait_ge(s_pool, 7)

            @block.scalar
            def _(act):
                for to, of in early_loads:
                    act.dma_start(to, of).then_inc(s_w, 16)
                deviation(act, 1, A)
                for to, of in late_loads[:4]:
                    act.dma_start(to, of).then_inc(s_late, 16)
                deviation(act, 2, B)
                for n, (a, b) in enumerate(CHUNKS):
                    act.wait_ge(s_tp, n + 1)
                    nc.scalar.copy(nodesT[0:D, a:b], pT[:, n % 2, 0:b - a]).then_inc(s_tc, 1)
                for to, of in late_loads[4:]:
                    act.dma_start(to, of).then_inc(s_late, 16)

            @block.vector
            def _(dve):
                nc.vector.memset(X[:, FULL_T, :], 0.0).then_inc(s_xpad, 1)
                dve.wait_ge(s_x, 16)
                link(dve, normalize(dve, X, H, T, 1, A))
                dve.wait_ge(s_w, 16 * len(early_loads))
                scale_shift(dve, H, 0, A).then_inc(s_h, 1)
                dve.wait_ge(s_wt, 1)
                nc.vector.tensor_copy(WkcT[:, :], pW[:, 0, 0:ZF])
                nc.vector.tensor_copy(WqT[:, :], pW[:, 0, P:P + D + 1])
                nc.vector.tensor_copy(mW2T[:, :], pW[0:D, 0, 2 * P:3 * P])
                nc.vector.tensor_copy(WvcT[:, :], pW[:, 1, 0:ZF]).then_inc(s_wtc, 1)
                link(dve, nc.vector.memset(U[:, :, :], 0.0))
                nc.vector.memset(U[ZF - 1:ZF, :, D:D + 1], 1.0)
                dve.wait_ge(s_wt, 2)
                for h in range(HEADS):
                    nc.vector.tensor_scalar(queryW[:, h, :], pW[0:D + 1, h, 0:ZF], float(D) ** -0.5, None, ALU.mult)
                    last = nc.vector.tensor_copy(U[:, h, 0:D], pW[0:ZF, h, P:P + D])
                last.then_inc(s_wp, 1)
                nc.vector.tensor_copy(cntW[:, :], pW[0:1, 1, 2 * P:3 * P])
                nc.vector.tensor_copy(msgW[:, :], pW[:, 0, 2 * P:3 * P]).then_inc(s_wp, 1)
                dve.wait_ge(s_x2, 32)
                link(dve, normalize(dve, X, H, T, 2, B))
                scale_shift(dve, H, 0, B).then_inc(s_h, 1)
                dve.wait_ge(s_dst, 16)
                link(dve, nc.vector.scalar_tensor_tensor(out=dst_real, in0=dst_rows, scalar=float(NO_NODE),
                                                         in1=dst_rows, op0=ALU.is_lt, op1=ALU.mult))
                nc.vector.tensor_reduce(lohi[:, 0, :], dst_rows, AX.X, ALU.min)
                nc.vector.tensor_reduce(lohi[:, 1, :], dst_real, AX.X, ALU.max).then_inc(s_lohi, 1)
                for n, (a, b) in enumerate(CHUNKS):
                    dve.wait_ge(s_qq, n + 1)
                    nc.vector.tensor_copy(queryT[0:ZF, a:b, :].rearrange("p n h -> p h n"),
                                          pS[0:ZF, n % 2, :, 0:b - a]).then_inc(s_qqc, 1)
                dve.wait_ge(s_lor, 16)
                link(dve, nc.vector.tensor_tensor(base_f[:, :], base0[:, 1, :], base0[:, 0, :], ALU.subtract))
                link(dve, nc.vector.tensor_reduce(span[:, 0:1], base_f[:, :], AX.X, ALU.max))
                link(dve, nc.vector.tensor_copy(rounds_i[:, 0:1], span[:, 0:1]))
                link(dve, nc.vector.tensor_scalar(rounds_i[:, 0:1], rounds_i[:, 0:1], W.bit_length() - 1, None,
                                                  ALU.arith_shift_right))
                nc.vector.tensor_scalar(rounds_i[:, 1:2], rounds_i[:, 0:1], 1.0, None, ALU.add)
                nc.vector.tensor_scalar(base_f[:, :], base0[:, 0, :], float(-W), None, ALU.add)

            @block.tensor
            def _(pe):
                pe.wait_ge(s_w, 16 * len(early_loads))
                pe.wait_ge(s_ident, 1)
                nc.tensor.transpose(pW[:, 0, 0:ZF], Wkc[:, :], ident[0:ZF, 0:ZF])
                nc.tensor.transpose(pW[:, 0, P:P + D + 1], WqB[:, :], ident[0:D + 1, 0:D + 1])
                nc.tensor.transpose(pW[0:D, 0, 2 * P:3 * P], mW2S[:, :], ident[:, :])
                nc.tensor.transpose(pW[:, 1, 0:ZF], Wvc[:, :], ident[0:ZF, 0:ZF]).then_inc(s_wt, 1)
                pe.wait_ge(s_wtc, 1)
                for h in range(HEADS):
                    c = slice(h * D, (h + 1) * D)
                    nc.tensor.matmul(pW[0:D + 1, h, 0:ZF], WqT[c, :], WkcT[c, :], start=True, stop=True)
                    nc.tensor.matmul(pW[0:ZF, h, P:P + D], WvcT[c, :], WpS[c, :], start=True, stop=True)
                nc.tensor.matmul(pW[:, 0, 2 * P:3 * P], mW2T[:, :], uWB[:, :], start=True, stop=True)
                nc.tensor.matmul(pW[0:1, 1, 2 * P:3 * P], mb2S[:, :], uWB[:, :], start=True,
                                 stop=True).then_inc(s_wt, 1)

                def turn_nodes(n):
                    a, b = CHUNKS[n]
                    pe.wait_ge(s_h, 1 if b <= PART * P else 2)
                    if n >= 2:
                        pe.wait_ge(s_tc, n - 1)
                    for t in range(a // P, b // P):
                        last = nc.tensor.transpose(pT[:, n % 2, t * P - a:t * P - a + P], H[:, t, :], ident[:, :])
                    last.then_inc(s_tp, 1)

                turn_nodes(0)
                pe.wait_ge(s_onerow, 1)
                pe.wait_ge(s_wp, 1)
                for n, (a, b) in enumerate(CHUNKS):
                    if n + 1 < len(CHUNKS):
                        turn_nodes(n + 1)
                    pe.wait_ge(s_tc, n + 1)
                    if n >= 2:
                        pe.wait_ge(s_qqc, n - 1)
                    for h in range(HEADS):
                        last = nc.tensor.matmul(pS[0:ZF, n % 2, h, 0:b - a], queryW[:, h, :], nodesT[0:D + 1, a:b],
                                                start=True, stop=True)
                    last.then_inc(s_qq, 1)

        s_gath1 = [sem(f"gathered_{i}") for i in range(RING)]
        s_gath2 = [sem(f"gathered_again_{i}") for i in range(RING)]
        s_base = sem("bases_ready")
        s_idx = [sem(f"sources_in_{i}") for i in range(RING)]
        s_tgt = [sem(f"targets_in_{i}") for i in range(RING)]
        s_ea = [sem(f"edge_features_in_{i}") for i in range(RING)]
        s_win = [sem(f"target_window_in_{i}") for i in range(RING)]
        s_turn = sem("gather_turn")
        s_zt = sem("rows_transposed")
        s_ztc = sem("rows_transpose_copied")
        s_sc = sem("scores_ready")
        s_other = sem("other_nodes_marked")
        s_sm = sem("scores_masked")
        s_smt = sem("scores_transposed")
        s_cm = sem("column_maxima")
        s_bc = sem("maxima_spread")
        s_fold = sem("scores_folded")
        s_mn = sem("new_maxima")
        s_bt = sem("best_updated")
        s_df = sem("old_maxima_read")
        s_xe = sem("exponents_ready")
        s_e = sem("weights_ready")
        s_agg = sem("window_summed")
        s_kept = sem("sum_rescaled")
        s_acc = sem("sum_updated")
        s_one = sem("targets_marked")
        s_pre = sem("hidden_product")
        s_hid = sem("hidden_ready")
        s_cnt = sem("counts_updated")
        loop_sems = [s_base, *s_idx, *s_tgt, *s_ea, *s_win, s_turn, s_zt, s_ztc, s_sc, s_other, s_sm, s_smt,
                     s_cm, s_bc, s_fold, s_mn, s_bt, s_df, s_xe, s_e, s_agg, s_kept, s_acc, s_one, s_pre, s_hid, s_cnt]
        numbers = [s.num for s in loop_sems]
        assert numbers == list(range(numbers[0], numbers[0] + len(numbers)))
        loop_range = range(numbers[0], numbers[-1] + 1)

        src_g = src.rearrange("(g p j) -> g p j", p=P, j=J)
        dst_g = dst.rearrange("(g p j) -> g p j", p=P, j=J)
        ea_g = ea.rearrange("(g p j) d -> g p j d", p=P, j=J)

        def bases_of(eng, g, n):
            return nc.values_load_multi_w_load_instructions(
                base_i[0:1, bass.ds(g, n)], engines=[eng.engine], min_val=0, max_val=LAST_BASE)[1]

        def next_bases(dve):
            nc.vector.tensor_scalar(base_f[:, :], base_f[:, :], float(W), float(LAST_BASE), ALU.add,
                                    ALU.min).then_inc(s_base, 1)
            dve.wait_ge(s_base, 1)
            nc.vector.tensor_copy(base_i[:, :], base_f[:, :]).then_inc(s_base, 1)

        def load_group(sp, it, off, wait, window, query=False):
            s = slot(off)
            if wait:
                sp.wait_ge(s_agg, at(it, off) - RING + 1)
            g = at(it, off)
            sp.dma_start(idx[:, s, :], src_g[bass.ds(g, 1), :, :].rearrange("g p j -> p (g j)")).then_inc(s_idx[s], 16)
            sp.dma_start(tgt[:, s, :], dst_g[bass.ds(g, 1), :, :].rearrange("g p j -> p (g j)")).then_inc(s_tgt[s], 16)
            sp.dma_start(z[:, s, :, D:D + ED],
                         ea_g[bass.ds(g, 1), :, :, :].rearrange("g p j d -> p (g j) d")).then_inc(s_ea[s], 16)
            if query:
                sp.dma_start(Qw[:, s, :, :], query_cols[:, bass.ds(window, W), :]).then_inc(s_win[s], 16)
            else:
                sp.dma_start(Wg[D + ED:P, s, :], target_rows[bass.ds(window, W), :]).then_inc(s_win[s], 16)

        def gathered(r, it, off):
            a_round = STEPS + (1 if slot(off) < G - STEPS * RING else 0)
            return 16 * J * (uses(it, off) + 1) + r * (16 * J * a_round)

        def gather_group(pool, it, off, s_gath):
            s = slot(off)
            pool.wait_ge(s_idx[s], 16 * (uses(it, off) + 1))
            nc.gpsimd.sem_inc(s_turn, 1)
            for j in range(J):
                nc.gpsimd.indirect_dma_start(
                    z[:, s, j, 0:D], None, source_rows[:, :],
                    bass.IndirectOffsetOnAxis(ap=idx[:, s, j:j + 1].bitcast(U32), axis=0)).then_inc(s_gath[s], 16)

        def all_groups(eng, do):
            for off in range(RING):
                do(0, off, False)
            with eng.Fori(1, STEPS) as it:
                for off in range(RING):
                    do(it, off, True)
            for off in range(G - STEPS * RING):
                do(STEPS, off, True)

        def load_all(sp, query):
            b = bases_of(nc.sync, 0, RING)
            for off in range(RING):
                load_group(sp, 0, off, False, b[off], query)
            with nc.sync.Fori(1, STEPS) as it:
                b = bases_of(nc.sync, at(it, 0), RING)
                for off in range(RING):
                    load_group(sp, it, off, True, b[off], query)
            b = bases_of(nc.sync, at(STEPS, 0), G - STEPS * RING)
            for off in range(G - STEPS * RING):
                load_group(sp, STEPS, off, True, b[off], query)

        rounds = nc.values_load(rounds_i[0:1, 1:2], min_val=1, max_val=NP // W)
        with psum("p_zt", [P, 2, GE]) as p_zt, psum("p_s", [P, HEADS, 2, J, W]) as p_s, \
                psum("p_smt", [P, CHUNK]) as p_smt, psum("p_bc", [P, CHUNK]) as p_bc, \
                psum("p_agg", [P, CHUNK]) as p_agg, nc.Fori(0, rounds) as r:
            with nc.Block() as block:

                @block.sync
                def _(sp):
                    sp.wait_ge(s_base, 2)
                    load_all(sp, True)

                @block.gpsimd
                def _(pool):
                    all_groups(nc.gpsimd, lambda it, off, free: gather_group(pool, it, off, s_gath1))

                @block.tensor
                def _(pe):
                    def transpose_rows(it, off, js):
                        s, g = slot(off), at(it, off)
                        if 0 in js:
                            pe.wait_ge(s_gath1[s], gathered(r, it, off))
                            pe.wait_ge(s_ea[s], 16 * (uses(it, off) + 1))
                            if past(it, off, 2):
                                pe.wait_ge(s_ztc, g - 1)
                        for j in js:
                            last = nc.tensor.transpose(p_zt[0:P, off % 2, j * P:(j + 1) * P], z[:, s, j, :],
                                                       ident[:, :])
                        if J - 1 in js:
                            last.then_inc(s_zt, 1)

                    def scores(it, off, js):
                        if 0 in js:
                            pe.wait_ge(s_win[slot(off)], 16 * (uses(it, off) + 1))
                            pe.wait_ge(s_ztc, at(it, off) + 1)
                        for j in js:
                            last = nc.tensor.matmul(p_s[:, :, 0, j, :], zT[0:ZF, off % 2, j * P:(j + 1) * P],
                                                    Qw[:, slot(off), :, :].rearrange("p n h -> p h n"),
                                                    start=True, stop=True)
                        if J - 1 in js:
                            last.then_inc(s_sc, 1)

                    def turn_scores(it, off):
                        pe.wait_ge(s_fold, at(it, off) + 1)
                        nc.tensor.transpose(p_smt[:, 0:P], folded[:, off % 2, :], ident[:, :]).then_inc(s_smt, 1)

                    def spread_maxima(it, off):
                        pe.wait_ge(s_cm, at(it, off) + 1)
                        nc.tensor.transpose(p_bc[:, 0:P], wide(colmax[:, off % 2:off % 2 + 1], [P, P]),
                                            ident[:, :]).then_inc(s_bc, 1)

                    def window_sums(it, off):
                        pe.wait_ge(s_e, at(it, off) + 1)
                        if past(it, off, 1):
                            pe.wait_ge(s_acc, at(it, off))
                        e = E[:, off % 2, 0:HEADS * J * W].rearrange("p (h j n) -> p h j n", h=HEADS, j=J)
                        for j in range(J):
                            last = nc.tensor.matmul(p_agg[0:ZF, 0:HW], z[:, slot(off), j, 0:ZF], e[:, :, j, :],
                                                    start=(j == 0), stop=(j == J - 1))
                        last.then_inc(s_agg, 1)

                    def turn(it, off, next_two=(True, True)):
                        turn_scores(it, off)
                        if next_two[0]:
                            scores(it, off + 1, [0])
                        if next_two[1]:
                            transpose_rows(it, off + 2, [0])
                        if next_two[0]:
                            scores(it, off + 1, [1])
                        spread_maxima(it, off)
                        if next_two[0]:
                            scores(it, off + 1, [2])
                        if next_two[1]:
                            transpose_rows(it, off + 2, [1])
                        if next_two[0]:
                            scores(it, off + 1, [3])
                        if next_two[1]:
                            transpose_rows(it, off + 2, [2, 3])
                        if past(it, off, 1):
                            window_sums(it, off - 1)

                    transpose_rows(0, 0, range(J))
                    scores(0, 0, range(J))
                    transpose_rows(0, 1, range(J))
                    for off in range(RING):
                        turn(0, off)
                    with nc.tensor.Fori(1, STEPS) as it:
                        for off in range(RING):
                            turn(it, off)
                    turn(STEPS, 0, next_two=(True, False))
                    turn(STEPS, 1, next_two=(False, False))
                    window_sums(STEPS, 1)

                @block.scalar
                def _(act):
                    def copy_rows(it, off):
                        act.wait_ge(s_zt, at(it, off) + 1)
                        if past(it, off, 2):
                            act.wait_ge(s_sc, at(it, off) - 1)
                        nc.scalar.copy(zT[0:ZF, off % 2, :], p_zt[0:ZF, off % 2, :]).then_inc(s_ztc, 1)

                    def weights(it, off):
                        act.wait_ge(s_xe, at(it, off) + 1)
                        nc.scalar.activation(E[:, off % 2, :], XE[:, off % 2, :], ACT.Exp).then_inc(s_e, 1)

                    copy_rows(0, 0)
                    copy_rows(0, 1)
                    with nc.scalar.Fori(0, STEPS) as it:
                        for off in range(RING):
                            weights(it, off)
                            copy_rows(it, off + 2)
                    weights(STEPS, 0)
                    weights(STEPS, 1)

                @block.vector
                def _(dve):
                    def mark_others(it, off, base):
                        s = slot(off)
                        dve.wait_ge(s_tgt[s], 16 * (uses(it, off) + 1))
                        nc.vector.tensor_tensor(
                            other[:, off % 2, :, :],
                            wide(node_id[:, bass.ds(base, W)].unsqueeze(1), [P, J, W]),
                            wide(tgt[:, s, :].unsqueeze(2), [P, J, W]), ALU.not_equal).then_inc(s_other, 1)

                    def mask_scores(it, off):
                        dve.wait_ge(s_other, at(it, off) + 1)
                        dve.wait_ge(s_sc, at(it, off) + 1)
                        nc.vector.scalar_tensor_tensor(
                            out=SM[:, off % 2, :, :, :].rearrange("p h j n -> p h (j n)"),
                            in0=wide(other[:, off % 2, :, :].rearrange("p j n -> p (j n)").unsqueeze(1),
                                     [P, HEADS, J * W]),
                            scalar=-FAR, in1=p_s[:, :, 0, :, :].rearrange("p h j n -> p h (j n)"),
                            op0=ALU.mult, op1=ALU.add).then_inc(s_sm, 1)
                        dve.wait_ge(s_sm, at(it, off) + 1)
                        nc.vector.tensor_reduce(folded[:, off % 2, 0:HW].rearrange("p (h n) -> p h n", h=HEADS),
                                                SM[:, off % 2, :, :, :].rearrange("p h j n -> p h n j"),
                                                AX.X, ALU.max).then_inc(s_fold, 1)

                    def column_maxima(it, off):
                        dve.wait_ge(s_smt, at(it, off) + 1)
                        nc.vector.tensor_reduce(colmax[:, off % 2:off % 2 + 1], p_smt[:, 0:P], AX.X,
                                                ALU.max).then_inc(s_cm, 1)

                    def new_maxima(it, off, base):
                        g = at(it, off)
                        old = best[:, :, bass.ds(base, W)]
                        now = p_bc[:, 0:HW].rearrange("p (h n) -> p h n", h=HEADS)
                        xe = XE[:, off % 2, :]
                        dve.wait_ge(s_bc, g + 1)
                        if past(it, off, 1):
                            dve.wait_ge(s_bt, g)
                        nc.vector.tensor_tensor(mnew[:, :, :], old, now, ALU.max).then_inc(s_mn, 1)
                        dve.wait_ge(s_mn, g + 1)
                        nc.vector.tensor_tensor(
                            xe[:, HEADS * J * W:].rearrange("p (h n) -> p h n", h=HEADS), old, mnew[:, :, :],
                            ALU.subtract).then_inc(s_df, 1)
                        nc.vector.tensor_tensor(
                            xe[:, 0:HEADS * J * W].rearrange("p (h j n) -> p h j n", h=HEADS, j=J),
                            SM[:, off % 2, :, :, :], wide(mnew[:, :, :].unsqueeze(2), [P, HEADS, J, W]),
                            ALU.subtract).then_inc(s_xe, 1)
                        dve.wait_ge(s_df, g + 1)
                        nc.vector.tensor_tensor(old, old, mnew[:, :, :], ALU.max).then_inc(s_bt, 1)

                    def add_sums(it, off, base):
                        g = at(it, off)
                        a = acc[0:ZF, :, bass.ds(base, W)]
                        dve.wait_ge(s_agg, g + 1)
                        if past(it, off, 1):
                            dve.wait_ge(s_acc, g)
                        nc.vector.tensor_tensor(
                            kept[0:ZF, :, :], a,
                            E[0:ZF, off % 2, HEADS * J * W:].rearrange("p (h n) -> p h n", h=HEADS),
                            ALU.mult).then_inc(s_kept, 1)
                        dve.wait_ge(s_kept, g + 1)
                        nc.vector.tensor_tensor(
                            a, kept[0:ZF, :, :], p_agg[0:ZF, 0:HW].rearrange("p (h n) -> p h n", h=HEADS),
                            ALU.add).then_inc(s_acc, 1)

                    def turn(it, off, b, last=False):
                        mask_scores(it, off)
                        b += bases_of(nc.vector, at(it, off - 2 + len(b)), (3 if last else 4) - len(b))
                        column_maxima(it, off)
                        add_sums(it, off - 2, b[0])
                        if not last:
                            mark_others(it, off + 1, b[3])
                        new_maxima(it, off, b[2])
                        return b[1:]

                    next_bases(dve)
                    dve.wait_ge(s_base, 2)
                    b = bases_of(nc.vector, 0, 3)
                    mark_others(0, 0, b[0])
                    for off in range(2):
                        mask_scores(0, off)
                        column_maxima(0, off)
                        mark_others(0, off + 1, b[off + 1])
                        new_maxima(0, off, b[off])
                    for off in range(2, RING + 2):
                        b = turn(0, off, b)
                    with nc.vector.Fori(1, STEPS - 1) as it:
                        b = []
                        for off in range(2, RING + 2):
                            b = turn(it, off, b)
                    b = []
                    for off in range(2, RING + 2):
                        b = turn(STEPS - 1, off, b, last=(off == RING + 1))
                    add_sums(STEPS, 0, b[0])
                    add_sums(STEPS, 1, b[1])

            nc.all_engine_barrier(sems_to_clear=loop_range)

        s_res = sem("residual_ready")
        s_o = sem("heads_product")
        s_od = sem("heads_joined")
        s_o2 = sem("attention_normalized")
        s_m1 = sem("mlp_first")
        s_m1c = sem("mlp_gelu")
        s_m2 = sem("mlp_second")
        s_m2c = sem("mlp_added")
        s_x1 = sem("first_layer_out")
        s_r = sem("target_product")
        s_rc = sem("target_copied")
        s_tab2 = sem("second_tables_out")
        s_c = sem("message_weights_in")
        T3 = 3
        OG = [(t, min(t + T3, NT)) for t in range(0, NT, T3)]
        OG_A = sum(b <= PART for _, b in OG)
        NC = len(CHUNKS)
        NC_A = sum(b <= PART * P for _, b in CHUNKS)
        with psum("p_o", [P, 3, CHUNK]) as p_o, psum("p_t", [D, 2, CHUNK]) as p_t, psum("p_m", [D, CHUNK]) as p_m, \
                psum("p_n", [P, 2, CHUNK]) as p_n, nc.Block() as block:

            @block.tensor
            def _(pe):
                for n, (a, b) in enumerate(OG):
                    if n >= 3:
                        pe.wait_ge(s_od, n - 2)
                    for t in range(a, b):
                        for h in range(HEADS):
                            c = ((t - a) * HEADS + h) * (D + 1)
                            last = nc.tensor.matmul(p_o[:, n % 3, c:c + D + 1], acc[0:ZF, h, t * P:(t + 1) * P],
                                                    U[:, h, :], start=True, stop=True)
                    last.then_inc(s_o, 1)

                def turn_nodes(k, of, ready):
                    a, b = CHUNKS[k % NC]
                    pe.wait_ge(ready, 1 if b <= PART * P else 2)
                    if k % NC >= 2:
                        pe.wait_ge(s_tc, k - 1)
                    for t in range(a // P, b // P):
                        last = nc.tensor.transpose(p_t[:, k % NC % 2, t * P - a:t * P - a + P], of[:, t, :],
                                                   ident[:, :])
                    last.then_inc(s_tp, 1)

                def first(n):
                    a, b = CHUNKS[n]
                    pe.wait_ge(s_tc, NC + n + 1)
                    if n >= 1:
                        pe.wait_ge(s_m1c, n)
                    nc.tensor.matmul(p_m[:, 0:b - a], W1B[:, :], nodesT[0:D + 1, a:b], start=True,
                                     stop=True).then_inc(s_m1, 1)

                def second(n):
                    a, b = CHUNKS[n]
                    pe.wait_ge(s_m1c, n + 1)
                    if n >= 2:
                        pe.wait_ge(s_m2c, n - 1)
                    for t in range(a // P, b // P):
                        last = nc.tensor.matmul(p_n[:, n % 2, t * D - a * D // P:(t + 1) * D - a * D // P],
                                                nodesT2[:, t * P:(t + 1) * P], W2B[:, :], start=True, stop=True)
                    last.then_inc(s_m2, 1)

                turn_nodes(NC, H, s_o2)
                first(0)
                for n in range(NC):
                    if n + 1 < NC:
                        turn_nodes(NC + n + 1, H, s_o2)
                    second(n)
                    if n + 1 < NC:
                        first(n + 1)
                turn_nodes(2 * NC, X, s_x1)
                for n, (a, b) in enumerate(CHUNKS):
                    if n + 1 < NC:
                        turn_nodes(2 * NC + n + 1, X, s_x1)
                    pe.wait_ge(s_tc, 2 * NC + n + 1)
                    if n >= 2:
                        pe.wait_ge(s_rc, n - 1)
                    else:
                        pe.wait_ge(s_m2c, NC)
                    for t in range(a // P, b // P):
                        last = nc.tensor.matmul(p_n[:, n % 2, t * P - a:(t + 1) * P - a],
                                                nodesT[0:D + 1, t * P:(t + 1) * P], mWB[:, :], start=True, stop=True)
                    last.then_inc(s_r, 1)

            @block.scalar
            def _(act):
                def turned(k):
                    a, b = CHUNKS[k % NC]
                    act.wait_ge(s_tp, k + 1)
                    nc.scalar.copy(nodesT[0:D, a:b], p_t[:, k % NC % 2, 0:b - a]).then_inc(s_tc, 1)

                def gelu(n):
                    a, b = CHUNKS[n]
                    act.wait_ge(s_m1, n + 1)
                    nc.scalar.activation(nodesT2[0:D, a:b], p_m[:, 0:b - a], ACT.Gelu).then_inc(s_m1c, 1)

                deviation(act, 3, A)
                turned(NC)
                for n in range(NC_A - 1):
                    turned(NC + n + 1)
                    gelu(n)
                deviation(act, 4, B)
                for n in range(NC_A - 1, NC):
                    if n + 1 < NC:
                        turned(NC + n + 1)
                    gelu(n)
                    if n == NC_A:
                        deviation(act, 5, A)
                deviation(act, 6, B)
                turned(2 * NC)
                for n, (a, b) in enumerate(CHUNKS):
                    if n + 1 < NC:
                        turned(2 * NC + n + 1)
                    act.wait_ge(s_r, n + 1)
                    nc.scalar.copy(R_out[:, a // P:b // P, :].rearrange("p t n -> p (t n)"),
                                   p_n[:, n % 2, 0:b - a]).then_inc(s_rc, 1)

            @block.vector
            def _(dve):
                def join_heads(n):
                    a, b = OG[n]
                    dve.wait_ge(s_o, n + 1)
                    o = p_o[:, n % 3, 0:(b - a) * HEADS * (D + 1)].rearrange("p (t h d) -> p t h d", h=HEADS, d=D + 1)
                    den = heads_den[:, a:b, :].unsqueeze(3)
                    num = heads_out[:, a:b, :, :]
                    link(dve, nc.vector.tensor_scalar(den, o[:, :, :, D:D + 1], 1e-8, None, ALU.add))
                    link(dve, nc.vector.reciprocal(den, den))
                    nc.vector.tensor_tensor(num, o[:, :, :, 0:D], wide(den, [P, b - a, HEADS, D]),
                                            ALU.mult).then_inc(s_od, 1)
                    dve.wait_ge(s_od, n + 1)
                    for h in range(HEADS):
                        link(dve, nc.vector.tensor_tensor(RES[:, a:b, :], RES[:, a:b, :], num[:, :, h, :], ALU.add))

                def add_mlp(n):
                    a, b = CHUNKS[n]
                    dve.wait_ge(s_m2, n + 1)
                    res = RES[:, a // P:b // P, :]
                    nc.vector.tensor_tensor(res, res,
                                            p_n[:, n % 2, 0:(b - a) // P * D].rearrange("p (t d) -> p t d", d=D),
                                            ALU.add).then_inc(s_m2c, 1)

                link(dve, nc.vector.tensor_tensor(RES[:, :, :], X[:, :, :], wide(rows[:, 4:5, :], [P, NT, D]),
                                                  ALU.add))
                for n in range(OG_A):
                    join_heads(n)
                link(dve, normalize(dve, RES, H, T, 3, A))
                scale_shift(dve, H, 2, A).then_inc(s_o2, 1)
                for n in range(OG_A, len(OG)):
                    join_heads(n)
                link(dve, normalize(dve, RES, H, T, 4, B))
                scale_shift(dve, H, 2, B).then_inc(s_o2, 1)
                link(dve, nc.vector.tensor_tensor(RES[:, :, :], RES[:, :, :], X[:, :, :], ALU.add))
                for n in range(NC_A):
                    add_mlp(n)
                dve.wait_ge(s_m2c, NC_A)
                normalize(dve, RES, X, T, 5, A).then_inc(s_x1, 1)
                for n in range(NC_A, NC):
                    add_mlp(n)
                dve.wait_ge(s_m2c, NC)
                normalize(dve, RES, X, T, 6, B).then_inc(s_x1, 1)
                nc.vector.tensor_scalar(base_f[:, :], base0[:, 0, :], float(-W), None, ALU.add)

            @block.gpsimd
            def _(pool):
                nc.gpsimd.memset(queryT[:, :, :], 0.0).then_inc(s_pool, 1)
                pool.wait_ge(s_pool, 8)
                nc.gpsimd.memset(cnt[:, :], 0.0)

            @block.sync
            def _(sp):
                for i in range(RING):
                    sp.dma_start(Wg[0:D, i, :], mW1[0:D, :]).then_inc(s_c, 16)
                    sp.dma_start(Wg[D:D + ED, i, :], mW1[2 * D:2 * D + ED, :]).then_inc(s_c, 16)
                tab, tgt_tab = (t.rearrange("(t p) d -> p t d", p=P) for t in (source_rows, target_rows))
                for n, part in enumerate((A, B)):
                    sp.wait_ge(s_x1, n + 1)
                    sp.dma_start(tab[:, part, :], X[:, part, :]).then_inc(s_tab2, 16)
                for n, (a, b) in enumerate(CHUNKS):
                    sp.wait_ge(s_rc, n + 1)
                    sp.dma_start(tgt_tab[:, a // P:b // P, :], R_out[:, a // P:b // P, :]).then_inc(s_tab2, 16)
                sp.wait_ge(s_c, 32 * RING)
                sp.wait_ge(s_tab2, 16 * (2 + NC))

        rounds2 = nc.values_load(rounds_i[0:1, 1:2], min_val=1, max_val=NP // W)
        with psum("p_zt2", [P, 2, GE]) as p_zt, psum("p_pre", [P, 2, J * HID]) as p_pre, \
                psum("p_sum", [P, 2, CHUNK]) as p_sum, psum("p_cnt", [P, 2, CHUNK]) as p_cnt, nc.Fori(0, rounds2) as r:
            with nc.Block() as block:

                @block.sync
                def _(sp):
                    sp.wait_ge(s_base, 2)
                    load_all(sp, False)

                @block.gpsimd
                def _(pool):
                    all_groups(nc.gpsimd, lambda it, off, free: gather_group(pool, it, off, s_gath2))

                @block.tensor
                def _(pe):
                    def transpose_rows(it, off):
                        s, g = slot(off), at(it, off)
                        pe.wait_ge(s_gath2[s], gathered(r, it, off))
                        pe.wait_ge(s_ea[s], 16 * (uses(it, off) + 1))
                        pe.wait_ge(s_one, g + 1)
                        if past(it, off, 2):
                            pe.wait_ge(s_ztc, g - 1)
                        for j in range(J):
                            last = nc.tensor.transpose(p_zt[:, off % 2, j * P:(j + 1) * P], z[:, s, j, :],
                                                       ident[:, :])
                        last.then_inc(s_zt, 1)

                    def hidden(it, off):
                        pe.wait_ge(s_ztc, at(it, off) + 1)
                        pe.wait_ge(s_win[slot(off)], 16 * (uses(it, off) + 1))
                        for j in range(J):
                            last = nc.tensor.matmul(p_pre[:, off % 2, j * HID:(j + 1) * HID],
                                                    zT[:, off % 2, j * P:(j + 1) * P], Wg[:, slot(off), :],
                                                    start=True, stop=True)
                        last.then_inc(s_pre, 1)

                    def window_sums(it, off):
                        g = at(it, off)
                        pe.wait_ge(s_hid, g + 1)
                        if past(it, off, 2):
                            pe.wait_ge(s_acc, g - 1)
                        mark = z[:, slot(off), :, D + ED:P]
                        for j in range(J):
                            nc.tensor.matmul(p_cnt[0:1, off % 2, 0:W], ones[:, :], mark[:, j, :],
                                             start=(j == 0), stop=(j == J - 1))
                        for j in range(J):
                            last = nc.tensor.matmul(p_sum[:, off % 2, 0:W], hid[:, off % 2, j, :], mark[:, j, :],
                                                    start=(j == 0), stop=(j == J - 1))
                        last.then_inc(s_agg, 1)

                    transpose_rows(0, 0)
                    transpose_rows(0, 1)
                    hidden(0, 0)
                    for off in range(1, RING + 1):
                        transpose_rows(0, off + 1)
                        hidden(0, off)
                        window_sums(0, off - 1)
                    with nc.tensor.Fori(1, STEPS) as it:
                        for off in range(1, RING + 1):
                            transpose_rows(it, off + 1)
                            hidden(it, off)
                            window_sums(it, off - 1)
                    hidden(STEPS, 1)
                    window_sums(STEPS, 0)
                    window_sums(STEPS, 1)

                @block.scalar
                def _(act):
                    def hidden_relu(it, off):
                        act.wait_ge(s_pre, at(it, off) + 1)
                        nc.scalar.activation(hid[:, off % 2, :, :].rearrange("p j n -> p (j n)"),
                                             p_pre[:, off % 2, :], ACT.Relu).then_inc(s_hid, 1)

                    hidden_relu(0, 0)
                    with nc.scalar.Fori(0, STEPS) as it:
                        for off in range(1, RING + 1):
                            hidden_relu(it, off)
                    hidden_relu(STEPS, 1)

                @block.vector
                def _(dve):
                    def mark_targets(it, off, base):
                        s = slot(off)
                        dve.wait_ge(s_tgt[s], 16 * (uses(it, off) + 1))
                        nc.vector.tensor_tensor(
                            z[:, s, :, D + ED:P], wide(node_id[:, bass.ds(base, W)].unsqueeze(1), [P, J, W]),
                            wide(tgt[:, s, :].unsqueeze(2), [P, J, W]), ALU.is_equal).then_inc(s_one, 1)

                    def copy_rows(it, off):
                        dve.wait_ge(s_zt, at(it, off) + 1)
                        if past(it, off, 2):
                            dve.wait_ge(s_pre, at(it, off) - 1)
                        nc.vector.tensor_copy(zT[:, off % 2, :], p_zt[:, off % 2, :]).then_inc(s_ztc, 1)

                    def add_sums(it, off, base):
                        g = at(it, off)
                        a, c = msgT[:, bass.ds(base, W)], cnt[:, bass.ds(base, W)]
                        dve.wait_ge(s_agg, g + 1)
                        if past(it, off, 1):
                            dve.wait_ge(s_acc, g)
                        nc.vector.tensor_tensor(c, c, p_cnt[0:1, off % 2, 0:W], ALU.add)
                        nc.vector.tensor_tensor(a, a, p_sum[:, off % 2, 0:W], ALU.add).then_inc(s_acc, 1)

                    def turn(it, off, b):
                        copy_rows(it, off + 1)
                        add_sums(it, off - 1, b[0])
                        mark_targets(it, off + 2, b[3])

                    next_bases(dve)
                    dve.wait_ge(s_base, 2)
                    b = bases_of(nc.vector, 0, 3)
                    for off in range(3):
                        mark_targets(0, off, b[off])
                    copy_rows(0, 0)
                    copy_rows(0, 1)
                    for off in range(1, RING + 1):
                        b = bases_of(nc.vector, off - 1, 4)
                        turn(0, off, b)
                    with nc.vector.Fori(1, STEPS - 1) as it:
                        b = bases_of(nc.vector, at(it, 0), RING + 3)
                        for off in range(1, RING + 1):
                            turn(it, off, b[off - 1:off + 3])
                    for off in range(1, RING):
                        b = bases_of(nc.vector, at(STEPS - 1, off - 1), 4)
                        turn(STEPS - 1, off, b)
                    b = bases_of(nc.vector, at(STEPS, -1), 3)
                    copy_rows(STEPS, 1)
                    add_sums(STEPS - 1, RING - 1, b[0])
                    add_sums(STEPS, 0, b[1])
                    add_sums(STEPS, 1, b[2])

            nc.all_engine_barrier(sems_to_clear=loop_range)

        s_cr = sem("counts_in_place")
        s_u1 = sem("update_first")
        s_u1c = sem("update_relu")
        s_u2 = sem("update_second")
        s_u2c = sem("update_added")
        s_y = sem("output_ready")
        s_out = sem("output_written")
        with psum("p_u", [P, 2, CHUNK]) as p_u, psum("p_v", [P, 2, CHUNK]) as p_v, nc.Block() as block:

            @block.tensor
            def _(pe):
                def first(n):
                    a, b = CHUNKS[n]
                    if n >= 2:
                        pe.wait_ge(s_u1c, n - 1)
                    nc.tensor.matmul(p_u[:, n % 2, 0:b - a], msgW[:, :], msgT[:, a:b], start=True, stop=False)
                    pe.wait_ge(s_cr, 16)
                    nc.tensor.matmul(p_u[:, n % 2, 0:b - a], uWA[:, :], nodesT[:, a:b], start=False,
                                     stop=True).then_inc(s_u1, 1)

                def second(n):
                    a, b = CHUNKS[n]
                    pe.wait_ge(s_u1c, n + 1)
                    if n >= 2:
                        pe.wait_ge(s_u2c, n - 1)
                    for t in range(a // P, b // P):
                        c = (t * P - a) * D // P
                        last = nc.tensor.matmul(p_v[:, n % 2, c:c + D], hidT[:, t * P:(t + 1) * P], uW2S[:, :],
                                                start=True, stop=True)
                    last.then_inc(s_u2, 1)

                first(0)
                for n in range(NC):
                    if n + 1 < NC:
                        first(n + 1)
                    second(n)

            @block.scalar
            def _(act):
                deviation(act, 7, A)
                deviation(act, 8, B)

            @block.vector
            def _(dve):
                def relu(n):
                    a, b = CHUNKS[n]
                    dve.wait_ge(s_u1, n + 1)
                    nc.vector.tensor_scalar(hidT[:, a:b], p_u[:, n % 2, 0:b - a], 0.0, None,
                                            ALU.max).then_inc(s_u1c, 1)

                def add_update(n):
                    a, b = CHUNKS[n]
                    dve.wait_ge(s_u2, n + 1)
                    res = RES[:, a // P:b // P, :]
                    nc.vector.tensor_tensor(res, res,
                                            p_v[:, n % 2, 0:(b - a) // P * D].rearrange("p (t d) -> p t d", d=D),
                                            ALU.add).then_inc(s_u2c, 1)

                link(dve, nc.vector.tensor_tensor(RES[:, :, :], X[:, :, :], wide(rows[:, 5:6, :], [P, NT, D]), ALU.add))
                relu(0)
                for n in range(NC):
                    if n + 1 < NC:
                        relu(n + 1)
                    add_update(n)
                    if n == NC_A:
                        dve.wait_ge(s_u2c, NC_A)
                        normalize(dve, RES, H, T, 7, A).then_inc(s_y, 1)
                dve.wait_ge(s_u2c, NC)
                normalize(dve, RES, H, T, 8, B).then_inc(s_y, 1)

            @block.sync
            def _(sp):
                sp.dma_start(nodesT[D + 1:D + 2, :], cnt[:, :]).then_inc(s_cr, 16)
                sp.wait_ge(s_y, 1)
                sp.dma_start(out[0:PART * P, :].rearrange("(t p) d -> p t d", p=P), H[:, A, :]).then_inc(s_out, 16)
                sp.wait_ge(s_y, 2)
                sp.dma_start(out[PART * P:FULL_T * P, :].rearrange("(t p) d -> p t d", p=P),
                             H[:, PART:FULL_T, :]).then_inc(s_out, 16)
                sp.dma_start(out[FULL_T * P:NODES, :], H[0:LAST_N, FULL_T, :]).then_inc(s_out, 16)
                sp.wait_ge(s_out, 48)


_INS = ['x', 'src', 'dst', 'edge_attr_32'] + ['L0_gnn_' + k for k in (
    'Wq bq Wk bk Wv bv We Wp bp ln1_g ln1_b ln2_g ln2_b W1 b1 W2 b2').split()] + ['L1_gnn_' + k for k in (
    'mW1 mb1 mW2 mb2 uW1 ub1 uW2 ub2').split()]
_PAD = {'src': 0, 'dst': NO_NODE, 'edge_attr_32': 0}


def kernel(**inputs):
    import numpy as _np
    import concourse.bacc as _bacc
    from concourse import mybir as _mybir
    from concourse.bass_utils import run_bass_kernel_spmd as _run

    nc = _bacc.Bacc("TRN2", target_bir_lowering=False, num_devices=1)
    arrays, args = {}, []
    for name in _INS:
        a = _np.ascontiguousarray(inputs[name])
        if name in _PAD:
            a = _np.concatenate([a, _np.full((EP - EDGES,) + a.shape[1:], _PAD[name], a.dtype)])
        arrays[f"in_{name}_dram"] = a
        args.append(nc.dram_tensor(f"in_{name}_dram", a.shape, _mybir.dt.from_np(a.dtype), kind="ExternalInput").ap())
    args.append(nc.dram_tensor("out_0_dram", (NODES, D), F32, kind="ExternalOutput").ap())
    build(nc, *args)
    r = _run(nc, [arrays], core_ids=[0])
    return r.results[0]["out_0_dram"]
```

```python
from contextlib import ExitStack

import concourse.bass as bass
from concourse import mybir

F32 = mybir.dt.float32
I32 = mybir.dt.int32
U32 = mybir.dt.uint32
ALU = mybir.AluOpType
ACT = mybir.ActivationFunctionType
AX = mybir.AxisListType

P = 128
NODES = 3125
EDGES = 103125
D = 64
ED = 32
HEADS = 2
HC = HEADS * D
HID = 128
EPS = 1e-5

NT = -(-NODES // P)
FULL_T = NODES // P
LAST_N = NODES - FULL_T * P
NP = NT * P
CHUNK = 512
PART = 12
A, B = slice(0, PART), slice(PART, NT)
PART2 = 16
A2, B2 = slice(0, PART2), slice(PART2, NT)
CHUNKS = [(c, min(c + CHUNK, NP)) for c in range(0, NP, CHUNK)]
NC = len(CHUNKS)
NC_A = sum(b <= PART * P for _, b in CHUNKS)
NC_A2 = sum(b <= PART2 * P for _, b in CHUNKS)

J = 4
GE = P * J
G = -(-EDGES // GE)
EP = G * GE
W = 32
NO_NODE = 1 << 20
LAST_BASE = NP - W
assert LAST_BASE >= NODES
HW = HEADS * W

RING = 10
STEPS = (G - 2) // RING
assert G == STEPS * RING + 2 and RING % 2 == 0

ZF = D + ED + 1
FAR = 1e30
NO_MAX = -1e20


def slot(off):
    return off % RING


def uses(it, off):
    return it + off // RING


def at(it, off):
    return it * RING + off


def past(it, off, n):
    return not isinstance(it, int) or at(it, off) >= n


def build(nc, x, src, dst, ea, Wq, bq, Wk, bk, Wv, bv, We, Wp, bp, ln1_g, ln1_b, ln2_g, ln2_b, W1, b1, W2, b2,
          mW1, mb1, mW2, mb2, uW1, ub1, uW2, ub2, out):
    with ExitStack() as ctx:
        def sb(name, shape, dt=F32):
            return ctx.enter_context(nc.sbuf_tensor(name, shape, dt))

        def sem(name):
            return ctx.enter_context(nc.semaphore(name))

        source_rows = nc.dram_tensor("source_rows", (NP, D), F32).ap()
        query_cols = nc.dram_tensor("query_cols", (ZF, NP, HEADS), F32).ap()
        target_rows = nc.dram_tensor("target_rows", (NP, HID), F32).ap()
        lohi_dram = nc.dram_tensor("lohi_dram", (2, G), F32).ap()

        ident = sb("ident", [P, P])
        ones = sb("ones", [P, 1])
        node_id = sb("node_id", [P, NP])
        X = sb("X", [P, NT, D])
        H = sb("H", [P, NT, D])
        T = sb("T", [P, NT, D])
        RES = sb("RES", [P, NT, D])
        stat = sb("stat", [P, 4, NT])
        rows = sb("rows", [P, 2, D])
        norm_cols = sb("norm_cols", [D, 4])
        norm_edge = sb("norm_edge", [ZF, ZF])
        norm_node = sb("norm_node", [D + 1, D + 1])
        norm_mlp = sb("norm_mlp", [D + 1, D + 1])
        nodesT = sb("nodesT", [D + 2, NP])
        nodesT2 = sb("nodesT2", [D + 1, NP])
        queryT = sb("queryT", [P, NP, HEADS])
        best = sb("best", [P, HEADS, NP])
        acc = sb("acc", [P, HEADS, NP])
        base0 = sb("base0", [1, 2, G])
        base_f = sb("base_f", [1, G])
        base_i = sb("base_i", [1, G], I32)
        lohi_sb = sb("lohi_sb", [G // 2, 2, 2])
        span = sb("span", [1, 2])
        rounds_i = sb("rounds_i", [1, 2], I32)
        WqB = sb("WqB", [D + 1, HC])
        Wkc = sb("Wkc", [ZF, HC])
        Wvc = sb("Wvc", [ZF, HC])
        WkcT = sb("WkcT", [P, ZF])
        WvcT = sb("WvcT", [P, ZF])
        WpS = sb("WpS", [P, D])
        U = sb("U", [ZF, HEADS, D + 1])
        W1B = sb("W1B", [D + 1, D])
        W1N = sb("W1N", [D + 1, D])
        W2B = sb("W2B", [D + 1, D])
        mWB = sb("mWB", [D + 1, HID])
        mW2S = sb("mW2S", [P, D])
        mW2T = sb("mW2T", [D, HID])
        mb2S = sb("mb2S", [D, 1])
        msgW = sb("msgW", [HID, HID])
        cntW = sb("cntW", [1, HID])
        uWA = sb("uWA", [D + 2, HID])
        WqT = sb("WqT", [P, D + 1])
        queryW = sb("queryW", [D + 1, HEADS, ZF])
        uWB = sb("uWB", [D, HID])
        uW2S = sb("uW2S", [P, D])
        idx = sb("idx", [P, RING, J], I32)
        tgt = sb("tgt", [P, RING, J], I32)
        z = sb("z", [P, RING, J, P])
        zT = sb("zT", [P, 2, GE])
        other = sb("other", [P, 2, J, W])
        SM = sb("SM", [P, 2, HEADS, J, W])
        folded = sb("folded", [P, 2, P])
        Qw = sb("Qw", [ZF, RING, W, HEADS])
        colmax = sb("colmax", [P, 2])
        mnew = sb("mnew", [P, HEADS, W])
        XE = sb("XE", [P, 2, HEADS * J * W + HW])
        E = sb("E", [P, 2, HEADS * J * W + HW])
        kept = sb("kept", [P, HEADS, W])
        Wg = sb("Wg", [P, RING, HID])
        hid = sb("hid", [P, 2, J, HID])

        heads_out = best[:, :, :].rearrange("p h n -> p (h n)")[:, 0:NT * HEADS * D].rearrange(
            "p (t h d) -> p t h d", t=NT, h=HEADS)
        heads_den = T[:, :, 0:HEADS]
        dst_rows = RES[:, :, :].rearrange("p t d -> p (t d)")[0:G // 2, 0:2 * GE].bitcast(I32).rearrange(
            "p (a e) -> p a e", a=2)
        dst_real = hid[:, :, :, :].rearrange("p a j n -> p (a j n)")[0:G // 2, :].rearrange("p (a e) -> p a e", a=2)
        lohi = lohi_sb[:, :, :]
        R_out = acc[:, 0, :].rearrange("p (t n) -> p t n", t=NT)
        queryT_flat = queryT[:, :, :].rearrange("p n h -> p (n h)")
        msgT = queryT_flat[:, 0:NP]
        hidT = queryT_flat[:, NP:]
        cnt = hidT[0:1, :]

        banks = ctx.enter_context(nc.psum_tensor("banks", [P, 8, CHUNK], F32))

        def wide(row, shape):
            return row.broadcast_to(shape)

        s_w = sem("weights_in")
        s_norm = sem("norm_weights_in")
        s_norm1 = sem("first_norm_matrices_ready")
        s_norm2 = sem("second_norm_matrix_ready")
        s_w1 = sem("mlp_weights_copied")
        s_late = sem("later_weights_in")
        s_wp = sem("weight_products_copied")
        s_x = sem("x_in")
        s_x2 = sem("x_second_part_in")
        s_xpad = sem("x_padding_zeroed")
        s_onerow = sem("ones_rows_set")
        s_ident0 = sem("ident_cleared")
        s_ident = sem("ident_ready")
        s_dve = sem("vector_step")
        s_pool = sem("gpsimd_step")
        s_var = sem("variance_ready")
        s_std = sem("deviation_ready")
        s_h = sem("normalized_ready")
        s_tp = sem("transposed")
        s_tc = sem("transpose_copied")
        s_qq = sem("score_product")
        s_qqc = sem("score_copied")
        s_wt = sem("weights_transposed")
        s_wtc = sem("weights_transpose_copied")
        s_dst = sem("dst_rows_in")
        s_lohi = sem("lohi_ready")
        s_lod = sem("lohi_out")
        s_lor = sem("lohi_row_in")
        s_source = sem("source_rows_out")
        s_tab = sem("query_cols_out")

        s_o = sem("heads_product")
        s_od = sem("heads_joined")
        s_o2 = sem("attention_normalized")
        s_m1 = sem("mlp_first")
        s_m1c = sem("mlp_gelu")
        s_m2 = sem("mlp_second")
        s_m2c = sem("mlp_added")
        s_x1 = sem("first_layer_out")
        s_r = sem("target_product")
        s_rc = sem("target_copied")
        s_tab2 = sem("target_rows_out")
        s_c = sem("message_weights_in")
        s_gath1 = [sem(f"gathered_{i}") for i in range(RING)]
        s_gath2 = [sem(f"gathered_again_{i}") for i in range(RING)]
        s_base = sem("bases_ready")
        s_idx = [sem(f"sources_in_{i}") for i in range(RING)]
        s_tgt = [sem(f"targets_in_{i}") for i in range(RING)]
        s_ea = [sem(f"edge_features_in_{i}") for i in range(RING)]
        s_win = [sem(f"target_window_in_{i}") for i in range(RING)]
        s_turn = sem("gather_turn")
        s_zt = sem("rows_transposed")
        s_ztc = sem("rows_transpose_copied")
        s_sc = sem("scores_ready")
        s_other = sem("other_nodes_marked")
        s_sm = sem("scores_masked")
        s_smt = sem("scores_transposed")
        s_cm = sem("column_maxima")
        s_bc = sem("maxima_spread")
        s_fold = sem("scores_folded")
        s_mn = sem("new_maxima")
        s_bt = sem("best_updated")
        s_df = sem("old_maxima_read")
        s_xe = sem("exponents_ready")
        s_e = sem("weights_ready")
        s_agg = sem("window_summed")
        s_kept = sem("sum_rescaled")
        s_acc = sem("sum_updated")
        s_one = sem("targets_marked")
        s_pre = sem("hidden_product")
        s_hid = sem("hidden_ready")
        loop_sems = [s_base, *s_idx, *s_tgt, *s_ea, *s_win, s_turn, s_zt, s_ztc, s_sc, s_other, s_sm, s_smt,
                     s_cm, s_bc, s_fold, s_mn, s_bt, s_df, s_xe, s_e, s_agg, s_kept, s_acc, s_one, s_pre, s_hid]
        numbers = [s.num for s in loop_sems]
        assert numbers == list(range(numbers[0], numbers[0] + len(numbers)))
        loop_range = range(numbers[0], numbers[-1] + 1)


        steps = [0]

        def link(eng, ins):
            steps[0] += 1
            ins.then_inc(s_dve, 1)
            eng.wait_ge(s_dve, steps[0])

        def center(dve, a, b, scratch, part):
            a, b, scratch = a[:, part, :], b[:, part, :], scratch[:, part, :]
            mean, sums, var = (stat[:, k, part] for k in range(3))
            link(dve, nc.vector.tensor_reduce(mean, a, AX.X, ALU.add))
            link(dve, nc.vector.tensor_scalar(mean, mean, 1.0 / D, None, ALU.mult))
            link(dve, nc.vector.tensor_tensor(b, a, wide(mean.unsqueeze(2), [P, part.stop - part.start, D]),
                                              ALU.subtract))
            link(dve, nc.vector.tensor_tensor(scratch, b, b, ALU.mult))
            link(dve, nc.vector.tensor_reduce(sums, scratch, AX.X, ALU.add))
            nc.vector.tensor_scalar(var, sums, 1.0 / D, EPS, ALU.mult, ALU.add).then_inc(s_var, 1)

        def rescale(dve, b, turn, part):
            dve.wait_ge(s_std, turn)
            link(dve, nc.vector.reciprocal(stat[:, 1, part], stat[:, 3, part]))
            b = b[:, part, :]
            return nc.vector.tensor_tensor(b, b, wide(stat[:, 1, part].unsqueeze(2),
                                                      [P, part.stop - part.start, D]), ALU.mult)

        def normalize(dve, a, b, scratch, turn, part):
            center(dve, a, b, scratch, part)
            return rescale(dve, b, turn, part)

        def deviation(act, turn, part):
            act.wait_ge(s_var, turn)
            nc.scalar.activation(stat[:, 3, part], stat[:, 2, part], ACT.Sqrt).then_inc(s_std, 1)

        def norm_matrix(dve, to, k, size):
            link(dve, nc.vector.tensor_copy(to[:, :], ident[0:size, 0:size]))
            link(dve, nc.vector.tensor_tensor(to[0:D, 0:D], to[0:D, 0:D], wide(norm_cols[:, k:k + 1], [D, D]),
                                              ALU.mult))
            return nc.vector.tensor_copy(to[0:D, size - 1:size], norm_cols[:, k + 1:k + 2])

        def line(v):
            return v.rearrange("(a n) -> a n", a=1)

        def spread(row):
            return row.rearrange("(a d) -> a d", a=1).partition_broadcast(P)

        norm_loads = [(norm_cols[:, k:k + 1], v.rearrange("(n a) -> n a", a=1))
                      for k, v in enumerate((ln1_g, ln1_b, ln2_g, ln2_b))]
        early_loads = [(WqB[0:D, :], Wq), (WqB[D:D + 1, :], line(bq)),
                       (Wkc[0:D, :], Wk), (Wkc[D:D + ED, :], We), (Wkc[D + ED:ZF, :], line(bk)),
                       (Wvc[0:D, :], Wv), (Wvc[D:D + ED, :], We), (Wvc[D + ED:ZF, :], line(bv)),
                       (WpS[:, :], Wp), (mW2S[:, :], mW2), (uWB[:, :], uW1[D:2 * D, :]),
                       (mb2S[:, :], mb2.rearrange("(n a) -> n a", a=1))]
        late_loads = [(W1B[0:D, :], W1), (W1B[D:D + 1, :], line(b1)), (W2B[0:D, :], W2), (W2B[D:D + 1, :], line(b2)),
                      (mWB[0:D, :], mW1[D:2 * D, :]), (mWB[D:D + 1, :], line(mb1)),
                      (uWA[0:D, :], uW1[0:D, :]), (uWA[D:D + 1, :], line(ub1)), (uW2S[:, :], uW2)]
        late_loads += [(rows[:, k, :], spread(r)) for k, r in ((0, bp), (1, ub2))]

        src_g = src.rearrange("(g p j) -> g p j", p=P, j=J)
        dst_g = dst.rearrange("(g p j) -> g p j", p=P, j=J)
        ea_g = ea.rearrange("(g p j) d -> g p j d", p=P, j=J)

        def bases_of(eng, g, n):
            return nc.values_load_multi_w_load_instructions(
                base_i[0:1, bass.ds(g, n)], engines=[eng.engine], min_val=0, max_val=LAST_BASE)[1]

        def next_bases(dve):
            nc.vector.tensor_scalar(base_f[:, :], base_f[:, :], float(W), float(LAST_BASE), ALU.add,
                                    ALU.min).then_inc(s_base, 1)
            dve.wait_ge(s_base, 1)
            nc.vector.tensor_copy(base_i[:, :], base_f[:, :]).then_inc(s_base, 1)

        def load_edges(sp, it, off, wait):
            s = slot(off)
            if wait:
                sp.wait_ge(s_agg, at(it, off) - RING + 1)
            g = at(it, off)
            sp.dma_start(idx[:, s, :], src_g[bass.ds(g, 1), :, :].rearrange("g p j -> p (g j)")).then_inc(s_idx[s], 16)
            sp.dma_start(tgt[:, s, :], dst_g[bass.ds(g, 1), :, :].rearrange("g p j -> p (g j)")).then_inc(s_tgt[s], 16)
            sp.dma_start(z[:, s, :, D:D + ED],
                         ea_g[bass.ds(g, 1), :, :, :].rearrange("g p j d -> p (g j) d")).then_inc(s_ea[s], 16)

        def load_window(sp, off, base, query):
            s = slot(off)
            if query:
                sp.dma_start(Qw[:, s, :, :], query_cols[:, bass.ds(base, W), :]).then_inc(s_win[s], 16)
            else:
                sp.dma_start(Wg[D + ED:P, s, :], target_rows[bass.ds(base, W), :]).then_inc(s_win[s], 16)

        def gathered(r, it, off):
            a_round = STEPS + (1 if slot(off) < G - STEPS * RING else 0)
            return 16 * J * (uses(it, off) + 1) + r * (16 * J * a_round)

        def gather_group(pool, it, off, s_gath):
            s = slot(off)
            pool.wait_ge(s_idx[s], 16 * (uses(it, off) + 1))
            nc.gpsimd.sem_inc(s_turn, 1)
            for j in range(J):
                nc.gpsimd.indirect_dma_start(
                    z[:, s, j, 0:D], None, source_rows[:, :],
                    bass.IndirectOffsetOnAxis(ap=idx[:, s, j:j + 1].bitcast(U32), axis=0)).then_inc(s_gath[s], 16)

        def gather_all(pool, s_gath):
            for off in range(RING):
                gather_group(pool, 0, off, s_gath)
            with nc.gpsimd.Fori(1, STEPS) as it:
                for off in range(RING):
                    gather_group(pool, it, off, s_gath)
            for off in range(G - STEPS * RING):
                gather_group(pool, STEPS, off, s_gath)

        def load_first_edges(sp):
            for off in range(RING):
                load_edges(sp, 0, off, False)

        def load_rest(sp, query, first):
            sp.wait_ge(s_base, 2)
            b = bases_of(nc.sync, 0, RING)
            if first and query:
                sp.wait_ge(s_tab, 16 * (1 + NC))
            elif first:
                sp.wait_ge(s_tab2, 16 * NC)
            for off in range(RING):
                load_window(sp, off, b[off], query)
            with nc.sync.Fori(1, STEPS) as it:
                b = bases_of(nc.sync, at(it, 0), RING)
                for off in range(RING):
                    load_edges(sp, it, off, True)
                    load_window(sp, off, b[off], query)
            b = bases_of(nc.sync, at(STEPS, 0), G - STEPS * RING)
            for off in range(G - STEPS * RING):
                load_edges(sp, STEPS, off, True)
                load_window(sp, off, b[off], query)

        p_zt = banks[:, 0:2, :]
        p_s = banks[:, 2, :].rearrange("p (h q j n) -> p h q j n", h=HEADS, q=2, j=J)
        p_smt, p_bc, p_agg = (banks[:, k, :] for k in (3, 4, 5))

        def first_edges_sync(sp, r, first):
            if not first:
                load_first_edges(sp)
            load_rest(sp, True, first)

        def first_edges_gpsimd(pool, r, first):
            if first:
                pool.wait_ge(s_source, 32)
            gather_all(pool, s_gath1)

        def first_edges_tensor(pe, r, first):
            def transpose_rows(it, off, js):
                s, g = slot(off), at(it, off)
                if 0 in js:
                    pe.wait_ge(s_gath1[s], gathered(r, it, off))
                    pe.wait_ge(s_ea[s], 16 * (uses(it, off) + 1))
                    if past(it, off, 2):
                        pe.wait_ge(s_ztc, g - 1)
                for j in js:
                    last = nc.tensor.transpose(p_zt[0:P, off % 2, j * P:(j + 1) * P], z[:, s, j, :],
                                               ident[:, :])
                if J - 1 in js:
                    last.then_inc(s_zt, 1)

            def scores(it, off, js):
                if 0 in js:
                    pe.wait_ge(s_win[slot(off)], 16 * (uses(it, off) + 1))
                    pe.wait_ge(s_ztc, at(it, off) + 1)
                for j in js:
                    last = nc.tensor.matmul(p_s[:, :, 0, j, :], zT[0:ZF, off % 2, j * P:(j + 1) * P],
                                            Qw[:, slot(off), :, :].rearrange("p n h -> p h n"),
                                            start=True, stop=True)
                if J - 1 in js:
                    last.then_inc(s_sc, 1)

            def turn_scores(it, off):
                pe.wait_ge(s_fold, at(it, off) + 1)
                nc.tensor.transpose(p_smt[:, 0:P], folded[:, off % 2, :], ident[:, :]).then_inc(s_smt, 1)

            def spread_maxima(it, off):
                pe.wait_ge(s_cm, at(it, off) + 1)
                nc.tensor.transpose(p_bc[:, 0:P], wide(colmax[:, off % 2:off % 2 + 1], [P, P]),
                                    ident[:, :]).then_inc(s_bc, 1)

            def window_sums(it, off):
                pe.wait_ge(s_e, at(it, off) + 1)
                if past(it, off, 1):
                    pe.wait_ge(s_acc, at(it, off))
                e = E[:, off % 2, 0:HEADS * J * W].rearrange("p (h j n) -> p h j n", h=HEADS, j=J)
                for j in range(J):
                    last = nc.tensor.matmul(p_agg[0:ZF, 0:HW], z[:, slot(off), j, 0:ZF], e[:, :, j, :],
                                            start=(j == 0), stop=(j == J - 1))
                last.then_inc(s_agg, 1)

            def turn(it, off, next_two=(True, True)):
                turn_scores(it, off)
                if next_two[0]:
                    scores(it, off + 1, [0])
                if next_two[1]:
                    transpose_rows(it, off + 2, [0])
                if next_two[0]:
                    scores(it, off + 1, [1])
                spread_maxima(it, off)
                if next_two[0]:
                    scores(it, off + 1, [2])
                if next_two[1]:
                    transpose_rows(it, off + 2, [1])
                if next_two[0]:
                    scores(it, off + 1, [3])
                if next_two[1]:
                    transpose_rows(it, off + 2, [2, 3])
                if past(it, off, 1):
                    window_sums(it, off - 1)

            if first:
                pe.wait_ge(s_tc, NC)
                pe.wait_ge(s_wp, 2)
                pe.wait_ge(s_qqc, NC)
            transpose_rows(0, 0, range(J))
            scores(0, 0, range(J))
            transpose_rows(0, 1, range(J))
            for off in range(RING):
                turn(0, off)
            with nc.tensor.Fori(1, STEPS) as it:
                for off in range(RING):
                    turn(it, off)
            turn(STEPS, 0, next_two=(True, False))
            turn(STEPS, 1, next_two=(False, False))
            window_sums(STEPS, 1)

        def first_edges_scalar(act, r, first):
            def copy_rows(it, off):
                act.wait_ge(s_zt, at(it, off) + 1)
                if past(it, off, 2):
                    act.wait_ge(s_sc, at(it, off) - 1)
                nc.scalar.copy(zT[0:ZF, off % 2, :], p_zt[0:ZF, off % 2, :]).then_inc(s_ztc, 1)

            def weights(it, off):
                act.wait_ge(s_xe, at(it, off) + 1)
                nc.scalar.activation(E[:, off % 2, :], XE[:, off % 2, :], ACT.Exp).then_inc(s_e, 1)

            copy_rows(0, 0)
            copy_rows(0, 1)
            with nc.scalar.Fori(0, STEPS) as it:
                for off in range(RING):
                    weights(it, off)
                    copy_rows(it, off + 2)
            weights(STEPS, 0)
            weights(STEPS, 1)

        def first_edges_vector(dve, r, first):
            def mark_others(it, off, base):
                s = slot(off)
                dve.wait_ge(s_tgt[s], 16 * (uses(it, off) + 1))
                nc.vector.tensor_tensor(
                    other[:, off % 2, :, :],
                    wide(node_id[:, bass.ds(base, W)].unsqueeze(1), [P, J, W]),
                    wide(tgt[:, s, :].unsqueeze(2), [P, J, W]), ALU.not_equal).then_inc(s_other, 1)

            def mask_scores(it, off):
                dve.wait_ge(s_other, at(it, off) + 1)
                dve.wait_ge(s_sc, at(it, off) + 1)
                nc.vector.scalar_tensor_tensor(
                    out=SM[:, off % 2, :, :, :].rearrange("p h j n -> p h (j n)"),
                    in0=wide(other[:, off % 2, :, :].rearrange("p j n -> p (j n)").unsqueeze(1),
                             [P, HEADS, J * W]),
                    scalar=-FAR, in1=p_s[:, :, 0, :, :].rearrange("p h j n -> p h (j n)"),
                    op0=ALU.mult, op1=ALU.add).then_inc(s_sm, 1)
                dve.wait_ge(s_sm, at(it, off) + 1)
                nc.vector.tensor_reduce(folded[:, off % 2, 0:HW].rearrange("p (h n) -> p h n", h=HEADS),
                                        SM[:, off % 2, :, :, :].rearrange("p h j n -> p h n j"),
                                        AX.X, ALU.max).then_inc(s_fold, 1)

            def column_maxima(it, off):
                dve.wait_ge(s_smt, at(it, off) + 1)
                nc.vector.tensor_reduce(colmax[:, off % 2:off % 2 + 1], p_smt[:, 0:P], AX.X,
                                        ALU.max).then_inc(s_cm, 1)

            def new_maxima(it, off, base):
                g = at(it, off)
                old = best[:, :, bass.ds(base, W)]
                now = p_bc[:, 0:HW].rearrange("p (h n) -> p h n", h=HEADS)
                xe = XE[:, off % 2, :]
                dve.wait_ge(s_bc, g + 1)
                if past(it, off, 1):
                    dve.wait_ge(s_bt, g)
                nc.vector.tensor_tensor(mnew[:, :, :], old, now, ALU.max).then_inc(s_mn, 1)
                dve.wait_ge(s_mn, g + 1)
                nc.vector.tensor_tensor(
                    xe[:, HEADS * J * W:].rearrange("p (h n) -> p h n", h=HEADS), old, mnew[:, :, :],
                    ALU.subtract).then_inc(s_df, 1)
                nc.vector.tensor_tensor(
                    xe[:, 0:HEADS * J * W].rearrange("p (h j n) -> p h j n", h=HEADS, j=J),
                    SM[:, off % 2, :, :, :], wide(mnew[:, :, :].unsqueeze(2), [P, HEADS, J, W]),
                    ALU.subtract).then_inc(s_xe, 1)
                dve.wait_ge(s_df, g + 1)
                nc.vector.tensor_tensor(old, old, mnew[:, :, :], ALU.max).then_inc(s_bt, 1)

            def add_sums(it, off, base):
                g = at(it, off)
                a = acc[0:ZF, :, bass.ds(base, W)]
                dve.wait_ge(s_agg, g + 1)
                if past(it, off, 1):
                    dve.wait_ge(s_acc, g)
                nc.vector.tensor_tensor(
                    kept[0:ZF, :, :], a,
                    E[0:ZF, off % 2, HEADS * J * W:].rearrange("p (h n) -> p h n", h=HEADS),
                    ALU.mult).then_inc(s_kept, 1)
                dve.wait_ge(s_kept, g + 1)
                nc.vector.tensor_tensor(
                    a, kept[0:ZF, :, :], p_agg[0:ZF, 0:HW].rearrange("p (h n) -> p h n", h=HEADS),
                    ALU.add).then_inc(s_acc, 1)

            def turn(it, off, b, last=False):
                mask_scores(it, off)
                b += bases_of(nc.vector, at(it, off - 2 + len(b)), (3 if last else 4) - len(b))
                column_maxima(it, off)
                add_sums(it, off - 2, b[0])
                if not last:
                    mark_others(it, off + 1, b[3])
                new_maxima(it, off, b[2])
                return b[1:]

            if first:
                dve.wait_ge(s_pool, 6)
            if not first:
                next_bases(dve)
            dve.wait_ge(s_base, 2)
            b = bases_of(nc.vector, 0, 3)
            mark_others(0, 0, b[0])
            for off in range(2):
                mask_scores(0, off)
                column_maxima(0, off)
                mark_others(0, off + 1, b[off + 1])
                new_maxima(0, off, b[off])
            for off in range(2, RING + 2):
                b = turn(0, off, b)
            with nc.vector.Fori(1, STEPS - 1) as it:
                b = []
                for off in range(2, RING + 2):
                    b = turn(it, off, b)
            b = []
            for off in range(2, RING + 2):
                b = turn(STEPS - 1, off, b, last=(off == RING + 1))
            add_sums(STEPS, 0, b[0])
            add_sums(STEPS, 1, b[1])

        pT, pW = banks[0:D, 0:2, :], banks[:, 2:4, :]
        pS = banks[:, 4:8, :].rearrange("p (a h) n -> p a h n", h=HEADS)
        with nc.Block() as block:

            @block.sync
            def _(sp):
                sp.dma_start(X[:, 0:PART, :], x[0:PART * P, :].rearrange("(t p) d -> p t d", p=P)).then_inc(s_x, 16)
                sp.dma_start(X[:, PART:FULL_T, :],
                             x[PART * P:FULL_T * P, :].rearrange("(t p) d -> p t d", p=P)).then_inc(s_x2, 16)
                sp.wait_ge(s_xpad, 1)
                sp.dma_start(X[0:LAST_N, FULL_T, :], x[FULL_T * P:NODES, :]).then_inc(s_x2, 16)
                for to, of in early_loads:
                    sp.dma_start(to, of).then_inc(s_w, 16)
                sp.dma_start(dst_rows, dst.rearrange("(p a e) -> p a e", a=2, e=GE)).then_inc(s_dst, 16)
                for off in range(2):
                    load_edges(sp, 0, off, False)
                tab = source_rows.rearrange("(t p) d -> p t d", p=P)
                sp.wait_ge(s_h, 1)
                sp.dma_start(tab[:, A, :], H[:, A, :]).then_inc(s_source, 16)
                sp.wait_ge(s_h, 2)
                sp.dma_start(tab[:, B, :], H[:, B, :]).then_inc(s_source, 16)
                for off in range(2, RING):
                    load_edges(sp, 0, off, False)
                sp.wait_ge(s_lohi, 1)
                for k in range(2):
                    sp.dma_start(lohi_dram[k, :].rearrange("(p a) -> p a", a=2), lohi[:, k, :]).then_inc(s_lod, 16)
                sp.wait_ge(s_lod, 32)
                sp.dma_start(base0[:, :, :], lohi_dram.rearrange("(o k) g -> o k g", o=1)).then_inc(s_lor, 16)
                sp.wait_ge(s_wp, 2)
                sp.dma_start(uWA[D + 1:D + 2, :], cntW[:, :]).then_inc(s_tab, 16)
                for n, (a, b) in enumerate(CHUNKS):
                    sp.wait_ge(s_qqc, n + 1)
                    sp.dma_start(query_cols[:, a:b, :], queryT[0:ZF, a:b, :]).then_inc(s_tab, 16)
                first_edges_sync(sp, 0, True)
                sp.wait_ge(s_late, 16 * len(late_loads))

            @block.gpsimd
            def _(pool):
                nc.gpsimd.memset(ident[:, :], 0.0).then_inc(s_ident0, 1)
                pool.wait_ge(s_ident0, 1)
                nc.gpsimd.affine_select(out=ident[:, :], in_=ident[:, :], compare_op=ALU.not_equal, fill=1.0, base=0,
                                        pattern=[[-1, P]], channel_multiplier=1).then_inc(s_ident, 1)
                pool.wait_ge(s_ident, 1)
                nc.gpsimd.memset(nodesT[D:D + 1, :], 1.0).then_inc(s_onerow, 1)
                pool.wait_ge(s_onerow, 1)
                nc.gpsimd.iota(node_id[:, :], [[1, NP]], base=0, channel_multiplier=0,
                               allow_small_or_imprecise_dtypes=True).then_inc(s_pool, 1)
                pool.wait_ge(s_pool, 1)
                nc.gpsimd.memset(z[:, :, :, D + ED:P], 1.0).then_inc(s_pool, 1)
                pool.wait_ge(s_pool, 2)
                nc.gpsimd.memset(folded[:, :, :], 0.0).then_inc(s_pool, 1)
                pool.wait_ge(s_pool, 3)
                nc.gpsimd.memset(best[:, :, :], NO_MAX).then_inc(s_pool, 1)
                pool.wait_ge(s_pool, 4)
                nc.gpsimd.memset(acc[:, :, :], 0.0).then_inc(s_pool, 1)
                pool.wait_ge(s_pool, 5)
                nc.gpsimd.memset(ones[:, :], 1.0).then_inc(s_pool, 1)
                pool.wait_ge(s_pool, 6)
                first_edges_gpsimd(pool, 0, True)

            @block.scalar
            def _(act):
                for to, of in norm_loads:
                    act.dma_start(to, of).then_inc(s_norm, 16)
                for to, of in late_loads[:4]:
                    act.dma_start(to, of).then_inc(s_late, 16)
                deviation(act, 1, A)
                deviation(act, 2, B)
                for n, (a, b) in enumerate(CHUNKS):
                    act.wait_ge(s_tp, n + 1)
                    nc.scalar.copy(nodesT[0:D, a:b], pT[:, n % 2, 0:b - a]).then_inc(s_tc, 1)
                for to, of in late_loads[4:]:
                    act.dma_start(to, of).then_inc(s_late, 16)
                first_edges_scalar(act, 0, True)

            @block.vector
            def _(dve):
                nc.vector.memset(X[:, FULL_T, :], 0.0).then_inc(s_xpad, 1)
                dve.wait_ge(s_x, 16)
                center(dve, X, H, T, A)
                dve.wait_ge(s_ident, 1)
                dve.wait_ge(s_norm, 64)
                norm_matrix(dve, norm_edge, 0, ZF)
                norm_matrix(dve, norm_node, 0, D + 1).then_inc(s_norm1, 1)
                dve.wait_ge(s_x2, 32)
                center(dve, X, H, T, B)
                dve.wait_ge(s_wt, 1)
                nc.vector.tensor_copy(WkcT[:, :], pW[:, 0, 0:ZF])
                nc.vector.tensor_copy(WqT[:, :], pW[:, 0, P:P + D + 1])
                nc.vector.tensor_copy(mW2T[:, :], pW[0:D, 0, 2 * P:3 * P])
                nc.vector.tensor_copy(WvcT[:, :], pW[:, 1, 0:ZF]).then_inc(s_wtc, 1)
                rescale(dve, H, 1, A).then_inc(s_h, 1)
                dve.wait_ge(s_wt, 2)
                for h in range(HEADS):
                    last = nc.vector.tensor_scalar(queryW[:, h, :], pW[0:D + 1, h, 0:ZF], float(D) ** -0.5, None,
                                                   ALU.mult)
                last.then_inc(s_wp, 1)
                rescale(dve, H, 2, B).then_inc(s_h, 1)
                norm_matrix(dve, norm_mlp, 2, D + 1).then_inc(s_norm2, 1)
                link(dve, nc.vector.memset(U[:, :, :], 0.0))
                nc.vector.memset(U[ZF - 1:ZF, :, D:D + 1], 1.0)
                for h in range(HEADS):
                    nc.vector.tensor_copy(U[:, h, 0:D], pW[0:ZF, h, P:P + D])
                nc.vector.tensor_copy(cntW[:, :], pW[0:1, 1, 2 * P:3 * P])
                nc.vector.tensor_copy(msgW[:, :], pW[:, 0, 2 * P:3 * P]).then_inc(s_wp, 1)
                dve.wait_ge(s_dst, 16)
                link(dve, nc.vector.scalar_tensor_tensor(out=dst_real, in0=dst_rows, scalar=float(NO_NODE),
                                                         in1=dst_rows, op0=ALU.is_lt, op1=ALU.mult))
                nc.vector.tensor_reduce(lohi[:, 0, :], dst_rows, AX.X, ALU.min)
                nc.vector.tensor_reduce(lohi[:, 1, :], dst_real, AX.X, ALU.max).then_inc(s_lohi, 1)
                for n, (a, b) in enumerate(CHUNKS):
                    if n == NC - 1:
                        dve.wait_ge(s_lor, 16)
                        link(dve, nc.vector.tensor_tensor(base_f[:, :], base0[:, 1, :], base0[:, 0, :], ALU.subtract))
                        link(dve, nc.vector.tensor_reduce(span[:, 0:1], base_f[:, :], AX.X, ALU.max))
                        link(dve, nc.vector.tensor_copy(rounds_i[:, 0:1], span[:, 0:1]))
                        link(dve, nc.vector.tensor_scalar(rounds_i[:, 0:1], rounds_i[:, 0:1], W.bit_length() - 1, None,
                                                          ALU.arith_shift_right))
                        nc.vector.tensor_scalar(rounds_i[:, 1:2], rounds_i[:, 0:1], 1.0, None, ALU.add)
                        link(dve, nc.vector.tensor_scalar(base_f[:, :], base0[:, 0, :], float(-W), None, ALU.add))
                        next_bases(dve)
                    dve.wait_ge(s_qq, n + 1)
                    nc.vector.tensor_copy(queryT[0:ZF, a:b, :].rearrange("p n h -> p h n"),
                                          pS[0:ZF, n % 2, :, 0:b - a]).then_inc(s_qqc, 1)
                first_edges_vector(dve, 0, True)

            @block.tensor
            def _(pe):
                pe.wait_ge(s_w, 16 * len(early_loads))
                pe.wait_ge(s_ident, 1)
                pe.wait_ge(s_norm1, 1)
                nc.tensor.matmul(pW[:, 0, 0:ZF], Wkc[:, :], norm_edge[:, :], start=True, stop=True)
                nc.tensor.matmul(pW[:, 0, P:P + D + 1], WqB[:, :], norm_node[:, :], start=True, stop=True)
                nc.tensor.transpose(pW[0:D, 0, 2 * P:3 * P], mW2S[:, :], ident[:, :])
                nc.tensor.matmul(pW[:, 1, 0:ZF], Wvc[:, :], norm_edge[:, :], start=True, stop=True).then_inc(s_wt, 1)
                pe.wait_ge(s_wtc, 1)
                for h in range(HEADS):
                    c = slice(h * D, (h + 1) * D)
                    nc.tensor.matmul(pW[0:D + 1, h, 0:ZF], WqT[c, :], WkcT[c, :], start=True, stop=True)
                    nc.tensor.matmul(pW[0:ZF, h, P:P + D], WvcT[c, :], WpS[c, :], start=True, stop=True)
                nc.tensor.matmul(pW[:, 0, 2 * P:3 * P], mW2T[:, :], uWB[:, :], start=True, stop=True)
                nc.tensor.matmul(pW[0:1, 1, 2 * P:3 * P], mb2S[:, :], uWB[:, :], start=True,
                                 stop=True).then_inc(s_wt, 1)

                def turn_nodes(n):
                    a, b = CHUNKS[n]
                    pe.wait_ge(s_h, 1 if b <= PART * P else 2)
                    if n >= 2:
                        pe.wait_ge(s_tc, n - 1)
                    for t in range(a // P, b // P):
                        last = nc.tensor.transpose(pT[:, n % 2, t * P - a:t * P - a + P], H[:, t, :], ident[:, :])
                    last.then_inc(s_tp, 1)

                turn_nodes(0)
                pe.wait_ge(s_onerow, 1)
                pe.wait_ge(s_wp, 1)
                for n, (a, b) in enumerate(CHUNKS):
                    if n + 1 < NC:
                        turn_nodes(n + 1)
                    pe.wait_ge(s_tc, n + 1)
                    if n >= 2:
                        pe.wait_ge(s_qqc, n - 1)
                    for h in range(HEADS):
                        last = nc.tensor.matmul(pS[0:ZF, n % 2, h, 0:b - a], queryW[:, h, :], nodesT[0:D + 1, a:b],
                                                start=True, stop=True)
                    last.then_inc(s_qq, 1)
                first_edges_tensor(pe, 0, True)

        nc.all_engine_barrier(sems_to_clear=loop_range)

        rounds = nc.values_load(rounds_i[0:1, 1:2], min_val=1, max_val=NP // W)
        with nc.If(rounds > 1):
            with nc.Fori(1, rounds) as r:
                with nc.Block() as block:

                    @block.sync
                    def _(sp):
                        first_edges_sync(sp, r, False)

                    @block.gpsimd
                    def _(pool):
                        first_edges_gpsimd(pool, r, False)

                    @block.tensor
                    def _(pe):
                        first_edges_tensor(pe, r, False)

                    @block.scalar
                    def _(act):
                        first_edges_scalar(act, r, False)

                    @block.vector
                    def _(dve):
                        first_edges_vector(dve, r, False)

                nc.all_engine_barrier(sems_to_clear=loop_range)

        p_pre, p_sum, p_cnt = banks[:, 2:4, :], banks[:, 4:6, :], banks[:, 6:8, :]

        def second_edges_sync(sp, r, first):
            if not first:
                load_first_edges(sp)
            load_rest(sp, False, first)

        def second_edges_gpsimd(pool, r, first):
            if first:
                pool.wait_ge(s_source, 64)
            gather_all(pool, s_gath2)

        def second_edges_tensor(pe, r, first):
            def transpose_rows(it, off, js):
                s, g = slot(off), at(it, off)
                if 0 in js:
                    pe.wait_ge(s_gath2[s], gathered(r, it, off))
                    pe.wait_ge(s_ea[s], 16 * (uses(it, off) + 1))
                    pe.wait_ge(s_one, g + 1)
                    if past(it, off, 2):
                        pe.wait_ge(s_ztc, g - 1)
                for j in js:
                    last = nc.tensor.transpose(p_zt[:, off % 2, j * P:(j + 1) * P], z[:, s, j, :], ident[:, :])
                if J - 1 in js:
                    last.then_inc(s_zt, 1)

            def hidden(it, off):
                pe.wait_ge(s_ztc, at(it, off) + 1)
                pe.wait_ge(s_win[slot(off)], 16 * (uses(it, off) + 1))
                for j in range(J):
                    last = nc.tensor.matmul(p_pre[:, off % 2, j * HID:(j + 1) * HID],
                                            zT[:, off % 2, j * P:(j + 1) * P], Wg[:, slot(off), :],
                                            start=True, stop=True)
                last.then_inc(s_pre, 1)

            def counts(it, off):
                if past(it, off, 2):
                    pe.wait_ge(s_acc, at(it, off) - 1)
                for j in range(J):
                    nc.tensor.matmul(p_cnt[0:1, off % 2, 0:W], ones[:, :], z[:, slot(off), j, D + ED:P],
                                     start=(j == 0), stop=(j == J - 1))

            def window_sums(it, off, js):
                if 0 in js:
                    pe.wait_ge(s_hid, at(it, off) + 1)
                for j in js:
                    last = nc.tensor.matmul(p_sum[:, off % 2, 0:W], hid[:, off % 2, j, :],
                                            z[:, slot(off), j, D + ED:P], start=(j == 0), stop=(j == J - 1))
                if J - 1 in js:
                    last.then_inc(s_agg, 1)

            def turn(it, off):
                transpose_rows(it, off + 1, [0, 1])
                counts(it, off - 1)
                window_sums(it, off - 1, [0])
                transpose_rows(it, off + 1, [2])
                window_sums(it, off - 1, [1])
                transpose_rows(it, off + 1, [3])
                window_sums(it, off - 1, [2, 3])
                hidden(it, off)

            if first:
                pe.wait_ge(s_m2c, NC)
                pe.wait_ge(s_rc, NC)
                pe.wait_ge(s_c, 32 * RING)
            transpose_rows(0, 0, range(J))
            transpose_rows(0, 1, range(J))
            hidden(0, 0)
            for off in range(1, RING + 1):
                turn(0, off)
            with nc.tensor.Fori(1, STEPS) as it:
                for off in range(1, RING + 1):
                    turn(it, off)
            counts(STEPS, 0)
            window_sums(STEPS, 0, range(J))
            hidden(STEPS, 1)
            counts(STEPS, 1)
            window_sums(STEPS, 1, range(J))

        def second_edges_scalar(act, r, first):
            def hidden_relu(it, off):
                act.wait_ge(s_pre, at(it, off) + 1)
                nc.scalar.activation(hid[:, off % 2, :, :].rearrange("p j n -> p (j n)"),
                                     p_pre[:, off % 2, :], ACT.Relu).then_inc(s_hid, 1)

            hidden_relu(0, 0)
            with nc.scalar.Fori(0, STEPS) as it:
                for off in range(1, RING + 1):
                    hidden_relu(it, off)
            hidden_relu(STEPS, 1)

        def second_edges_vector(dve, r, first):
            def mark_targets(it, off, base):
                s = slot(off)
                dve.wait_ge(s_tgt[s], 16 * (uses(it, off) + 1))
                nc.vector.tensor_tensor(
                    z[:, s, :, D + ED:P], wide(node_id[:, bass.ds(base, W)].unsqueeze(1), [P, J, W]),
                    wide(tgt[:, s, :].unsqueeze(2), [P, J, W]), ALU.is_equal).then_inc(s_one, 1)

            def copy_rows(it, off):
                dve.wait_ge(s_zt, at(it, off) + 1)
                if past(it, off, 2):
                    dve.wait_ge(s_pre, at(it, off) - 1)
                nc.vector.tensor_copy(zT[:, off % 2, :], p_zt[:, off % 2, :]).then_inc(s_ztc, 1)

            def add_sums(it, off, base):
                g = at(it, off)
                a, c = msgT[:, bass.ds(base, W)], cnt[:, bass.ds(base, W)]
                dve.wait_ge(s_agg, g + 1)
                if past(it, off, 1):
                    dve.wait_ge(s_acc, g)
                nc.vector.tensor_tensor(c, c, p_cnt[0:1, off % 2, 0:W], ALU.add)
                nc.vector.tensor_tensor(a, a, p_sum[:, off % 2, 0:W], ALU.add).then_inc(s_acc, 1)

            def turn(it, off, b):
                copy_rows(it, off + 1)
                mark_targets(it, off + 2, b[3])
                add_sums(it, off - 1, b[0])

            if first:
                dve.wait_ge(s_pool, 8)
            if not first:
                next_bases(dve)
            dve.wait_ge(s_base, 2)
            b = bases_of(nc.vector, 0, 3)
            for off in range(3):
                mark_targets(0, off, b[off])
            copy_rows(0, 0)
            copy_rows(0, 1)
            for off in range(1, RING + 1):
                b = bases_of(nc.vector, off - 1, 4)
                turn(0, off, b)
            with nc.vector.Fori(1, STEPS - 1) as it:
                b = bases_of(nc.vector, at(it, 0), RING + 3)
                for off in range(1, RING + 1):
                    turn(it, off, b[off - 1:off + 3])
            for off in range(1, RING):
                b = bases_of(nc.vector, at(STEPS - 1, off - 1), 4)
                turn(STEPS - 1, off, b)
            b = bases_of(nc.vector, at(STEPS, -1), 3)
            copy_rows(STEPS, 1)
            add_sums(STEPS - 1, RING - 1, b[0])
            add_sums(STEPS, 0, b[1])
            add_sums(STEPS, 1, b[2])

        T3 = 3
        OG = [(t, min(t + T3, NT)) for t in range(0, NT, T3)]
        OG_A = sum(b <= PART for _, b in OG)
        p_o, p_t, p_n = banks[:, 0:3, :], banks[0:D, 3:5, :], banks[:, 5:7, :]
        p_m = (banks[0:D, 7, :], p_o[0:D, 0, :])
        p_s2 = [banks[:, k, :] for k in (5, 6, 1, 2)]
        OG_P_M = max(n for n in range(len(OG)) if n % 3 == 0) + 1
        with nc.Block() as block:

            @block.tensor
            def _(pe):
                pe.wait_ge(s_norm2, 1)
                nc.tensor.matmul(banks[0:D + 1, 7, 0:D], norm_mlp[:, :], W1B[:, :], start=True,
                                 stop=True).then_inc(s_w1, 1)
                for n, (a, b) in enumerate(OG):
                    if n >= 3:
                        pe.wait_ge(s_od, n - 2)
                    for t in range(a, b):
                        for h in range(HEADS):
                            c = ((t - a) * HEADS + h) * (D + 1)
                            last = nc.tensor.matmul(p_o[:, n % 3, c:c + D + 1], acc[0:ZF, h, t * P:(t + 1) * P],
                                                    U[:, h, :], start=True, stop=True)
                    last.then_inc(s_o, 1)

                def turn_nodes(k, of, ready, part=PART):
                    a, b = CHUNKS[k % NC]
                    pe.wait_ge(ready, 1 if b <= part * P else 2)
                    if k % NC >= 2:
                        pe.wait_ge(s_tc, k - 1)
                    for t in range(a // P, b // P):
                        last = nc.tensor.transpose(p_t[:, k % NC % 2, t * P - a:t * P - a + P], of[:, t, :],
                                                   ident[:, :])
                    last.then_inc(s_tp, 1)

                def first(n):
                    a, b = CHUNKS[n]
                    pe.wait_ge(s_tc, NC + n + 1)
                    if n >= 2:
                        pe.wait_ge(s_m1c, n - 1)
                    if n == 0:
                        pe.wait_ge(s_w1, 2)
                    if n == 1:
                        pe.wait_ge(s_od, OG_P_M)
                    nc.tensor.matmul(p_m[n % 2][:, 0:b - a], W1N[:, :], nodesT[0:D + 1, a:b], start=True,
                                     stop=True).then_inc(s_m1, 1)

                def second(n):
                    a, b = CHUNKS[n]
                    pe.wait_ge(s_m1c, n + 1)
                    if n == 2:
                        pe.wait_ge(s_od, len(OG))
                    if n >= 4:
                        pe.wait_ge(s_m2c, n - 3)
                    for t in range(a // P, b // P):
                        last = nc.tensor.matmul(p_s2[n % 4][:, t * D - a * D // P:(t + 1) * D - a * D // P],
                                                nodesT2[:, t * P:(t + 1) * P], W2B[:, :], start=True, stop=True)
                    last.then_inc(s_m2, 1)

                pe.wait_ge(s_pool, 7)
                for part in (range(0, NC_A), range(NC_A, NC)):
                    turn_nodes(NC + part[0], H, s_o2)
                    for n in part:
                        if n + 1 in part:
                            turn_nodes(NC + n + 1, H, s_o2)
                        first(n)
                        if n - 1 in part:
                            second(n - 1)
                    second(part[-1])
                turn_nodes(2 * NC, X, s_x1, PART2)
                for n, (a, b) in enumerate(CHUNKS):
                    if n + 1 < NC:
                        turn_nodes(2 * NC + n + 1, X, s_x1, PART2)
                    pe.wait_ge(s_tc, 2 * NC + n + 1)
                    if n >= 2:
                        pe.wait_ge(s_rc, n - 1)
                    else:
                        pe.wait_ge(s_m2c, NC)
                    for t in range(a // P, b // P):
                        last = nc.tensor.matmul(p_n[:, n % 2, t * P - a:(t + 1) * P - a],
                                                nodesT[0:D + 1, t * P:(t + 1) * P], mWB[:, :], start=True, stop=True)
                    last.then_inc(s_r, 1)
                second_edges_tensor(pe, 0, True)

            @block.scalar
            def _(act):
                def turned(k):
                    a, b = CHUNKS[k % NC]
                    act.wait_ge(s_tp, k + 1)
                    nc.scalar.copy(nodesT[0:D, a:b], p_t[:, k % NC % 2, 0:b - a]).then_inc(s_tc, 1)

                def gelu(n):
                    a, b = CHUNKS[n]
                    act.wait_ge(s_m1, n + 1)
                    nc.scalar.activation(nodesT2[0:D, a:b], p_m[n % 2][:, 0:b - a], ACT.Gelu).then_inc(s_m1c, 1)

                act.wait_ge(s_w1, 1)
                nc.scalar.copy(W1N[:, :], banks[0:D + 1, 7, 0:D]).then_inc(s_w1, 1)
                deviation(act, 3, A)
                for n in range(NC_A):
                    turned(NC + n)
                    if n >= 1:
                        gelu(n - 1)
                gelu(NC_A - 1)
                deviation(act, 4, B)
                turned(NC + NC_A)
                for n in range(NC_A, NC):
                    if n + 1 < NC:
                        turned(NC + n + 1)
                    gelu(n)
                deviation(act, 5, A2)
                deviation(act, 6, B2)
                turned(2 * NC)
                for n, (a, b) in enumerate(CHUNKS):
                    if n + 1 < NC:
                        turned(2 * NC + n + 1)
                    act.wait_ge(s_r, n + 1)
                    nc.scalar.copy(R_out[:, a // P:b // P, :].rearrange("p t n -> p (t n)"),
                                   p_n[:, n % 2, 0:b - a]).then_inc(s_rc, 1)
                second_edges_scalar(act, 0, True)

            @block.vector
            def _(dve):
                def join_heads(n):
                    a, b = OG[n]
                    dve.wait_ge(s_o, n + 1)
                    o = p_o[:, n % 3, 0:(b - a) * HEADS * (D + 1)].rearrange("p (t h d) -> p t h d", h=HEADS, d=D + 1)
                    den = heads_den[:, a:b, :].unsqueeze(3)
                    num = heads_out[:, a:b, :, :]
                    link(dve, nc.vector.tensor_scalar(den, o[:, :, :, D:D + 1], 1e-8, None, ALU.add))
                    link(dve, nc.vector.reciprocal(den, den))
                    nc.vector.tensor_tensor(num, o[:, :, :, 0:D], wide(den, [P, b - a, HEADS, D]),
                                            ALU.mult).then_inc(s_od, 1)
                    dve.wait_ge(s_od, n + 1)
                    for h in range(HEADS):
                        link(dve, nc.vector.tensor_tensor(RES[:, a:b, :], RES[:, a:b, :], num[:, :, h, :], ALU.add))

                def add_mlp(n):
                    a, b = CHUNKS[n]
                    dve.wait_ge(s_m2, n + 1)
                    res = RES[:, a // P:b // P, :]
                    nc.vector.tensor_tensor(res, res,
                                            p_s2[n % 4][:, 0:(b - a) // P * D].rearrange("p (t d) -> p t d", d=D),
                                            ALU.add).then_inc(s_m2c, 1)

                link(dve, nc.vector.tensor_tensor(RES[:, :, :], X[:, :, :], wide(rows[:, 0:1, :], [P, NT, D]),
                                                  ALU.add))
                for n in range(OG_A):
                    join_heads(n)
                normalize(dve, RES, H, T, 3, A).then_inc(s_o2, 1)
                for n in range(OG_A, len(OG)):
                    join_heads(n)
                normalize(dve, RES, H, T, 4, B).then_inc(s_o2, 1)
                link(dve, nc.vector.tensor_scalar(base_f[:, :], base0[:, 0, :], float(-W), None, ALU.add))
                next_bases(dve)
                link(dve, nc.vector.tensor_tensor(RES[:, :, :], RES[:, :, :], X[:, :, :], ALU.add))
                for n in range(NC_A2):
                    add_mlp(n)
                dve.wait_ge(s_m2c, NC_A2)
                center(dve, RES, X, T, A2)
                for n in range(NC_A2, NC):
                    add_mlp(n)
                dve.wait_ge(s_m2c, NC)
                rescale(dve, X, 5, A2).then_inc(s_x1, 1)
                center(dve, RES, X, T, B2)
                rescale(dve, X, 6, B2).then_inc(s_x1, 1)
                second_edges_vector(dve, 0, True)

            @block.gpsimd
            def _(pool):
                nc.gpsimd.memset(nodesT2[D:D + 1, :], 1.0).then_inc(s_pool, 1)
                pool.wait_ge(s_pool, 7)
                nc.gpsimd.memset(queryT[:, :, :], 0.0).then_inc(s_pool, 1)
                pool.wait_ge(s_pool, 8)
                second_edges_gpsimd(pool, 0, True)

            @block.sync
            def _(sp):
                load_first_edges(sp)
                for i in range(RING):
                    sp.dma_start(Wg[0:D, i, :], mW1[0:D, :]).then_inc(s_c, 16)
                    sp.dma_start(Wg[D:D + ED, i, :], mW1[2 * D:2 * D + ED, :]).then_inc(s_c, 16)
                tab, tgt_tab = (t.rearrange("(t p) d -> p t d", p=P) for t in (source_rows, target_rows))
                for n, part in enumerate((A2, B2)):
                    sp.wait_ge(s_x1, n + 1)
                    sp.dma_start(tab[:, part, :], X[:, part, :]).then_inc(s_source, 16)
                for n, (a, b) in enumerate(CHUNKS):
                    sp.wait_ge(s_rc, n + 1)
                    sp.dma_start(tgt_tab[:, a // P:b // P, :], R_out[:, a // P:b // P, :]).then_inc(s_tab2, 16)
                second_edges_sync(sp, 0, True)

        nc.all_engine_barrier(sems_to_clear=loop_range)

        rounds = nc.values_load(rounds_i[0:1, 1:2], min_val=1, max_val=NP // W)
        with nc.If(rounds > 1):
            with nc.Fori(1, rounds) as r:
                with nc.Block() as block:

                    @block.sync
                    def _(sp):
                        second_edges_sync(sp, r, False)

                    @block.gpsimd
                    def _(pool):
                        second_edges_gpsimd(pool, r, False)

                    @block.tensor
                    def _(pe):
                        second_edges_tensor(pe, r, False)

                    @block.scalar
                    def _(act):
                        second_edges_scalar(act, r, False)

                    @block.vector
                    def _(dve):
                        second_edges_vector(dve, r, False)

                nc.all_engine_barrier(sems_to_clear=loop_range)

        s_cr = sem("counts_in_place")
        s_u1 = sem("update_first")
        s_u1c = sem("update_relu")
        s_u2 = sem("update_second")
        s_u2c = sem("update_added")
        s_y = sem("output_ready")
        s_out = sem("output_written")
        p_u, p_v = banks[:, 0:4, :], banks[:, 4:8, :]
        with nc.Block() as block:

            @block.tensor
            def _(pe):
                def messages(n):
                    a, b = CHUNKS[n]
                    if n >= 4:
                        pe.wait_ge(s_u1c, n - 3)
                    nc.tensor.matmul(p_u[:, n % 4, 0:b - a], msgW[:, :], msgT[:, a:b], start=True, stop=False)

                def nodes(n):
                    a, b = CHUNKS[n]
                    pe.wait_ge(s_cr, 16)
                    nc.tensor.matmul(p_u[:, n % 4, 0:b - a], uWA[:, :], nodesT[:, a:b], start=False,
                                     stop=True).then_inc(s_u1, 1)

                def second(n):
                    a, b = CHUNKS[n]
                    pe.wait_ge(s_u1c, n + 1)
                    if n >= 4:
                        pe.wait_ge(s_u2c, n - 3)
                    for t in range(a // P, b // P):
                        c = (t * P - a) * D // P
                        last = nc.tensor.matmul(p_v[:, n % 4, c:c + D], hidT[:, t * P:(t + 1) * P], uW2S[:, :],
                                                start=True, stop=True)
                    last.then_inc(s_u2, 1)

                for n in range(3):
                    messages(n)
                nodes(0)
                for n in range(NC):
                    if n + 3 < NC:
                        messages(n + 3)
                    if n + 1 < NC:
                        nodes(n + 1)
                    second(n)

            @block.scalar
            def _(act):
                for n, (a, b) in enumerate(CHUNKS):
                    act.wait_ge(s_u1, n + 1)
                    nc.scalar.activation(hidT[:, a:b], p_u[:, n % 4, 0:b - a], ACT.Relu).then_inc(s_u1c, 1)
                deviation(act, 7, A2)
                deviation(act, 8, B2)

            @block.vector
            def _(dve):
                def add_update(n):
                    a, b = CHUNKS[n]
                    dve.wait_ge(s_u2, n + 1)
                    res = RES[:, a // P:b // P, :]
                    nc.vector.tensor_tensor(res, res,
                                            p_v[:, n % 4, 0:(b - a) // P * D].rearrange("p (t d) -> p t d", d=D),
                                            ALU.add).then_inc(s_u2c, 1)

                link(dve, nc.vector.tensor_tensor(RES[:, :, :], X[:, :, :], wide(rows[:, 1:2, :], [P, NT, D]), ALU.add))
                for n in range(NC):
                    add_update(n)
                    if n == NC_A2 - 1:
                        dve.wait_ge(s_u2c, NC_A2)
                        center(dve, RES, H, T, A2)
                dve.wait_ge(s_u2c, NC)
                rescale(dve, H, 7, A2).then_inc(s_y, 1)
                center(dve, RES, H, T, B2)
                rescale(dve, H, 8, B2).then_inc(s_y, 1)

            @block.sync
            def _(sp):
                sp.dma_start(nodesT[D + 1:D + 2, :], cnt[:, :]).then_inc(s_cr, 16)
                sp.wait_ge(s_y, 1)
                sp.dma_start(out[0:PART2 * P, :].rearrange("(t p) d -> p t d", p=P), H[:, A2, :]).then_inc(s_out, 16)
                sp.wait_ge(s_y, 2)
                sp.dma_start(out[PART2 * P:FULL_T * P, :].rearrange("(t p) d -> p t d", p=P),
                             H[:, PART2:FULL_T, :]).then_inc(s_out, 16)
                sp.dma_start(out[FULL_T * P:NODES, :], H[0:LAST_N, FULL_T, :]).then_inc(s_out, 16)
                sp.wait_ge(s_out, 48)


_INS = ['x', 'src', 'dst', 'edge_attr_32'] + ['L0_gnn_' + k for k in (
    'Wq bq Wk bk Wv bv We Wp bp ln1_g ln1_b ln2_g ln2_b W1 b1 W2 b2').split()] + ['L1_gnn_' + k for k in (
    'mW1 mb1 mW2 mb2 uW1 ub1 uW2 ub2').split()]
_PAD = {'src': 0, 'dst': NO_NODE, 'edge_attr_32': 0}


def kernel(**inputs):
    import numpy as _np
    import concourse.bacc as _bacc
    from concourse import mybir as _mybir
    from concourse.bass_utils import run_bass_kernel_spmd as _run

    nc = _bacc.Bacc("TRN2", target_bir_lowering=False, num_devices=1)
    arrays, args = {}, []
    for name in _INS:
        a = _np.ascontiguousarray(inputs[name])
        if name in _PAD:
            a = _np.concatenate([a, _np.full((EP - EDGES,) + a.shape[1:], _PAD[name], a.dtype)])
        arrays[f"in_{name}_dram"] = a
        args.append(nc.dram_tensor(f"in_{name}_dram", a.shape, _mybir.dt.from_np(a.dtype), kind="ExternalInput").ap())
    args.append(nc.dram_tensor("out_0_dram", (NODES, D), F32, kind="ExternalOutput").ap())
    build(nc, *args)
    r = _run(nc, [arrays], core_ids=[0])
    return r.results[0]["out_0_dram"]
```
